# Optimizing a Trainium2 kernel written in Bass

```python
import numpy as np
import jax
import jax.numpy as jnp

def _softmax(x, axis=-1):
    return jax.nn.softmax(x, axis=axis)

def _gelu(x):
    return jax.nn.gelu(x, approximate=True)

def _silu(x):
    return jax.nn.silu(x)

def _sigmoid(x):
    return jax.nn.sigmoid(x)

def _layernorm(x, axis=-1, eps=1e-05):
    m = jnp.mean(x, axis=axis, keepdims=True)
    v = jnp.var(x, axis=axis, keepdims=True)
    return (x - m) / jnp.sqrt(v + eps)

def _scatter_add(tgt, idx, src, axis=0):
    return tgt.at[idx].add(src)

def _segment_sum(src, seg, n):
    return jax.ops.segment_sum(src, seg, n)
kernel_name = 'mk_macaron_d1_jaxref_r8_f2414e'

def setup_inputs(seed: int=0):
    np.random.seed(seed)
    _w = jnp.asarray

    def _L0_attn_setup():
        import jax, jax.numpy as jnp
        import numpy as np
        import math
        B, T, E, H, DQ, NB, MAXLEN = (4, 128, 128, 16, 64, 10, 128)
        NEG = -1000000000.0

        def _attn_forward(X, Wq, bq, Wk, Wv, Wproj, bproj, Wr, br, b_nd):
            b, t, e = X.shape
            maxlen = b_nd.shape[1]
            nb = b_nd.shape[0]
            h = H
            dq = Wq.shape[1] // h
            Q = (X @ Wq + bq).reshape(b, t, h, dq).transpose(0, 2, 1, 3)
            K = (X @ Wk).reshape(b, t, h, dq).transpose(0, 2, 1, 3)
            V = (X @ Wv).reshape(b, t, h, dq).transpose(0, 2, 1, 3)
            R = (X @ Wr + br).reshape(b, t, h, nb).transpose(0, 2, 1, 3)
            d = jnp.arange(t)[:, None] - jnp.arange(t)[None, :]
            valid = (d >= 0) & (d < maxlen)
            bias = jnp.where(valid, 0.0, NEG).astype(jnp.float32)
            D_ntT = jnp.where(valid[None, :, :], b_nd[:, jnp.clip(d, 0, maxlen - 1)], 0.0)
            extra = jnp.einsum('bhtn,ntp->bhtp', R, D_ntT)
            logits = jnp.einsum('bhtd,bhpd->bhtp', Q, K) / math.sqrt(dq) + bias + extra
            W = jax.nn.softmax(logits, axis=-1)
            A = jnp.einsum('bhtp,bhpd->bhtd', W, V)
            A = A.transpose(0, 2, 1, 3).reshape(b, t, h * dq)
            return A @ Wproj + bproj
        key = jax.random.key(seed)
        k = jax.random.split(key, 10)
        X = jax.random.normal(k[0], (B, T, E), jnp.float32)
        Wq = jax.random.normal(k[1], (E, H * DQ), jnp.float32) * (0.1 / math.sqrt(E))
        bq = jnp.zeros((H * DQ,), jnp.float32)
        Wk = jax.random.normal(k[2], (E, H * DQ), jnp.float32) * (0.2 / math.sqrt(E))
        Wv = jax.random.normal(k[3], (E, H * DQ), jnp.float32) * (1.0 / math.sqrt(E))
        Wproj = jax.random.normal(k[4], (H * DQ, E), jnp.float32) * (1.0 / math.sqrt(H * DQ))
        bproj = jnp.zeros((E,), jnp.float32)
        Wr = jax.random.normal(k[5], (E, H * NB), jnp.float32) * (0.1 / math.sqrt(E))
        br = jnp.zeros((H * NB,), jnp.float32)
        b_nd = jax.random.normal(k[6], (NB, MAXLEN), jnp.float32) * 0.2
        return dict(X=X, Wq=Wq, bq=bq, Wk=Wk, Wv=Wv, Wproj=Wproj, bproj=bproj, Wr=Wr, br=br, b_nd=b_nd)
    _L0_attn_in = _L0_attn_setup()

    def _L0_ffn_setup():
        import jax, jax.numpy as jnp
        import numpy as np
        B, S, D = (2, 256, 128)
        M = 256
        E = 8
        TOP_K = 2
        key = jax.random.key(seed)
        ks = jax.random.split(key, 5)
        std = 0.02
        return {'residual': jax.random.normal(ks[0], (B, S, D), jnp.float32), 'W_router': jax.random.normal(ks[1], (D, E), jnp.float32) * std, 'W_gate': jax.random.normal(ks[2], (E, D, M), jnp.float32) * std, 'b_gate': jnp.zeros((E, M), jnp.float32), 'W_up': jax.random.normal(ks[3], (E, D, M), jnp.float32) * std, 'b_up': jnp.zeros((E, M), jnp.float32), 'W_out': jax.random.normal(ks[4], (E, M, D), jnp.float32) * std, 'b_out': jnp.zeros((E, D), jnp.float32)}
    _L0_ffn_in = _L0_ffn_setup()
    _d = {'L0_attn_X': _L0_attn_in['X'], 'L0_attn_Wq': _L0_attn_in['Wq'], 'L0_attn_bq': _L0_attn_in['bq'], 'L0_attn_Wk': _L0_attn_in['Wk'], 'L0_attn_Wv': _L0_attn_in['Wv'], 'L0_attn_Wproj': _L0_attn_in['Wproj'], 'L0_attn_bproj': _L0_attn_in['bproj'], 'L0_attn_Wr': _L0_attn_in['Wr'], 'L0_attn_br': _L0_attn_in['br'], 'L0_attn_b_nd': _L0_attn_in['b_nd'], 'L0_ffn_W_router': _L0_ffn_in['W_router'], 'L0_ffn_W_gate': _L0_ffn_in['W_gate'], 'L0_ffn_b_gate': _L0_ffn_in['b_gate'], 'L0_ffn_W_up': _L0_ffn_in['W_up'], 'L0_ffn_b_up': _L0_ffn_in['b_up'], 'L0_ffn_W_out': _L0_ffn_in['W_out'], 'L0_ffn_b_out': _L0_ffn_in['b_out']}
    _x0 = _d['L0_attn_X']
    _d['L0_attn_X'] = jax.random.normal(jax.random.fold_in(jax.random.key(seed), 1), (1, 2048, 128), dtype=_x0.dtype)
    del _x0
    return _d

def reference(L0_attn_X, L0_attn_Wq, L0_attn_bq, L0_attn_Wk, L0_attn_Wv, L0_attn_Wproj, L0_attn_bproj, L0_attn_Wr, L0_attn_br, L0_attn_b_nd, L0_ffn_W_router, L0_ffn_W_gate, L0_ffn_b_gate, L0_ffn_W_up, L0_ffn_b_up, L0_ffn_W_out, L0_ffn_b_out):

    def _L0_attn_ref(X, Wq, bq, Wk, Wv, Wproj, bproj, Wr, br, b_nd):
        import jax, jax.numpy as jnp
        import numpy as np
        import math
        B, T, E, H, DQ, NB, MAXLEN = (4, 128, 128, 16, 64, 10, 128)
        NEG = -1000000000.0

        def _attn_forward(X, Wq, bq, Wk, Wv, Wproj, bproj, Wr, br, b_nd):
            b, t, e = X.shape
            maxlen = b_nd.shape[1]
            nb = b_nd.shape[0]
            h = H
            dq = Wq.shape[1] // h
            Q = (X @ Wq + bq).reshape(b, t, h, dq).transpose(0, 2, 1, 3)
            K = (X @ Wk).reshape(b, t, h, dq).transpose(0, 2, 1, 3)
            V = (X @ Wv).reshape(b, t, h, dq).transpose(0, 2, 1, 3)
            R = (X @ Wr + br).reshape(b, t, h, nb).transpose(0, 2, 1, 3)
            d = jnp.arange(t)[:, None] - jnp.arange(t)[None, :]
            valid = (d >= 0) & (d < maxlen)
            bias = jnp.where(valid, 0.0, NEG).astype(jnp.float32)
            D_ntT = jnp.where(valid[None, :, :], b_nd[:, jnp.clip(d, 0, maxlen - 1)], 0.0)
            extra = jnp.einsum('bhtn,ntp->bhtp', R, D_ntT)
            logits = jnp.einsum('bhtd,bhpd->bhtp', Q, K) / math.sqrt(dq) + bias + extra
            W = jax.nn.softmax(logits, axis=-1)
            A = jnp.einsum('bhtp,bhpd->bhtd', W, V)
            A = A.transpose(0, 2, 1, 3).reshape(b, t, h * dq)
            return A @ Wproj + bproj
        return _attn_forward(X, Wq, bq, Wk, Wv, Wproj, bproj, Wr, br, b_nd)

    def _L0_ffn_ref(residual, W_router, W_gate, b_gate, W_up, b_up, W_out, b_out):
        import jax, jax.numpy as jnp
        import numpy as np
        B, S, D = (2, 256, 128)
        M = 256
        E = 8
        TOP_K = 2
        router_logits = jnp.einsum('bsd,de->bse', residual, W_router)
        router_probs = jax.nn.softmax(router_logits, axis=-1)
        top_k_probs, top_k_idx = jax.lax.top_k(router_probs, TOP_K)
        top_k_probs = top_k_probs / (jnp.sum(top_k_probs, -1, keepdims=True) + 1e-08)
        one_hot = jax.nn.one_hot(top_k_idx, E, dtype=residual.dtype)
        expert_weights = jnp.einsum('bsk,bske->bse', top_k_probs, one_hot)
        gate = jax.nn.silu(jnp.einsum('bsd,edm->ebsm', residual, W_gate) + b_gate[:, None, None, :])
        up = jnp.einsum('bsd,edm->ebsm', residual, W_up) + b_up[:, None, None, :]
        hidden = gate * up
        expert_out = jnp.einsum('ebsm,emd->ebsd', hidden, W_out) + b_out[:, None, None, :]
        output = jnp.einsum('bse,ebsd->bsd', expert_weights, expert_out)
        return output
    x = L0_attn_X
    x = x + 0.5 * _L0_ffn_ref(_layernorm(x, axis=-1), L0_ffn_W_router, L0_ffn_W_gate, L0_ffn_b_gate, L0_ffn_W_up, L0_ffn_b_up, L0_ffn_W_out, L0_ffn_b_out)
    x = x + _L0_attn_ref(_layernorm(x, axis=-1), L0_attn_Wq, L0_attn_bq, L0_attn_Wk, L0_attn_Wv, L0_attn_Wproj, L0_attn_bproj, L0_attn_Wr, L0_attn_br, L0_attn_b_nd)
    x = x + 0.5 * _L0_ffn_ref(_layernorm(x, axis=-1), L0_ffn_W_router, L0_ffn_W_gate, L0_ffn_b_gate, L0_ffn_W_up, L0_ffn_b_up, L0_ffn_W_out, L0_ffn_b_out)
    return x

_drawn_inputs = setup_inputs


def setup_inputs(seed=0):
    import zlib

    import numpy as np

    out = dict(_drawn_inputs(seed))
    spreads = {'L0_attn_bq': (0.0, 0.8),
     'L0_attn_bproj': (0.0, 0.1),
     'L0_attn_br': (0.0, 0.8),
     'L0_ffn_b_gate': (0.0, 0.8),
     'L0_ffn_b_up': (0.0, 0.8),
     'L0_ffn_b_out': (0.0, 0.1)}
    factors = {'L0_attn_Wq': 8.0,
     'L0_attn_Wk': 8.0,
     'L0_attn_Wr': 8.0,
     'L0_attn_b_nd': 6.09,
     'L0_ffn_W_gate': 8.0,
     'L0_ffn_W_up': 8.0,
     'L0_ffn_W_out': 7.955}
    for name, (base, spread) in spreads.items():
        noise = np.random.default_rng([zlib.crc32(name.encode()), seed]).standard_normal(out[name].shape)
        drawn = base * np.exp(spread * noise) if base else spread * noise
        out[name] = jnp.asarray(drawn.astype(out[name].dtype))
    for name, factor in factors.items():
        out[name] = (out[name] * factor).astype(out[name].dtype)
    return out
```

```python
from contextlib import ExitStack

import concourse.bass as bass
from concourse import mybir

ALU = mybir.AluOpType
ACT = mybir.ActivationFunctionType
F32 = mybir.dt.float32
F32R = mybir.dt.float32r
X = mybir.AxisListType.X

P = 128
T, D = 2048, 128
GT = 512
NGROUP = T // GT
NBLK = GT // P
E, M = 8, 256
NCH = E * M // P
H, DQ, NB = 16, 64, 10
NPAIR = H // 2
NQ = 4 * NBLK
NP = 2 * NQ
NH = 4 * NQ
NOUT = 24
LAG = 2
NEG = -1.0e9
EPS = 1.0e-5

USES_SETUP = ["bias"]
USES_ROUTE = ["x", "route", "w"]
USES_TAIL1 = ["y", "x"]
USES_TAIL2 = ["z", "x", "route", "w"]
USES_ATT_LAST = [f"e{q}" for q in range(4, NQ)]
USES_ATT = ["e4", "e5", "e6", "e7", "x", "e8", "e9", "route", "e10", "e11", "e12", "e13", "w", "e14", "e15"]
USES_QKV0 = ["r0", "r1", "r2", "r3", "e0", "e1", "e2", "e3"]
USES_QKV = ["r0", "r1", "r2", "r3", "y", "e0", "e1", "e2", "e3"]
ORDER_PROLOGUE = [("setup", USES_SETUP), ("route", USES_ROUTE), ("ffn2", USES_TAIL1), ("qkv", USES_QKV0)]
ORDER_LOOP = [("att", USES_ATT), ("ffn1", USES_TAIL2), ("ffn2", USES_TAIL1), ("qkv", USES_QKV)]
ORDER_LAST = [("att", USES_ATT_LAST), ("ffn1", USES_TAIL2), ("end", ["y"])]
N_PROLOGUE = sum(len(u) for _, u in ORDER_PROLOGUE)
N_LOOP = sum(len(u) for _, u in ORDER_LOOP)
MISC_X_STEP, MISC_ROUTE_STEP, MISC_W_STEP = 4, 6, 10


def misc_use(where, g, stage, use):
    order, base = {"pro": (ORDER_PROLOGUE, 0), "loop": (ORDER_LOOP, g * N_LOOP + N_PROLOGUE),
                   "last": (ORDER_LAST, (NGROUP - 1) * N_LOOP + N_PROLOGUE)}[where]
    for name, uses in order:
        if name == stage:
            return base + uses.index(use)
        base = base + len(uses)
    raise KeyError(stage)


def band_uses(g, q):
    return g * 6 + (1 if q < 4 else 1 + q // 4)


def weight_uses(where, g, second):
    return 0 if where == "pro" else g * 6 + 5 + (1 if second and where == "loop" else 0)


def macaron(nc, x_in, wq, bq, wk, wv, wproj, bproj, wr, br, brev, wrt, wg, bg, wu, bu, wo, bo, out):
    with ExitStack() as ctx:
        def sb(name, shape, dt=F32):
            return ctx.enter_context(nc.sbuf_tensor(name, shape, dt))

        def sem(name):
            return ctx.enter_context(nc.semaphore(name))

        skew = nc.dram_tensor("skew", (4, 4 * P * 2 * P), F32, kind="Internal").ap()
        wd = nc.dram_tensor("wd", (2, E * GT), F32, kind="Internal").ap()

        bank = [ctx.enter_context(nc.psum_tensor(f"bank{i}", [P, 512], F32)) for i in range(8)]
        acc, misc, ptb = bank[4], bank[5], bank[6:8]

        gu_hi, gu_lo = sb("gu_hi", [P, E, 2, M], F32R), sb("gu_lo", [P, E, 2, M], F32R)
        qkv_hi, qkv_lo = sb("qkv_hi", [P, 3, H * DQ], F32R), sb("qkv_lo", [P, 3, H * DQ], F32R)
        r_hi, r_lo = sb("r_hi", [P, 4, P], F32R), sb("r_lo", [P, 4, P], F32R)
        rt_hi, rt_lo = sb("rt_hi", [P, E], F32R), sb("rt_lo", [P, E], F32R)
        b_hi, b_lo = sb("b_hi", [P, 4 * P], F32R), sb("b_lo", [P, 4 * P], F32R)
        wo_s, wp_s, bo_s = sb("wo_s", [P, NCH, D]), sb("wp_s", [P, NPAIR, D]), sb("bo_s", [E, D])
        bias = sb("bias", [P, 48])
        x0, x1, x2 = (sb(f"x{i}", [P, NBLK, D]) for i in range(3))
        xn = sb("xn", [P, NBLK, D])
        xh = [sb("xh_a", [P, GT], F32R), sb("xh_b", [P, GT], F32R)]
        xl = [sb("xl_a", [P, GT], F32R), sb("xl_b", [P, GT], F32R)]
        yz = xn[:, :, :].rearrange("p t d -> p (t d)")
        qt, kt, vt = sb("qt", [P, NPAIR, GT]), sb("kt", [P, NPAIR, GT + P]), sb("vt", [P, NBLK + 1, H * DQ])
        rs = sb("rs", [P, 4, GT], F32R)
        es = sb("es", [P, 2, 4 * P])
        wide = sb("wide", [P, 4, 4 * 2 * P])
        work = sb("work", [P, 6144])
        lg_s = [work[:, 256 * i:256 * i + 256] for i in range(4)]
        ex_s = [work[:, 1024 + 512 * i:1536 + 512 * i] for i in range(4)]
        pn_s = [work[:, 3072 + 512 * i:3584 + 512 * i] for i in range(4)]
        pt_s = [work[:, 5120 + 512 * i:5632 + 512 * i] for i in range(2)]
        sg_s = [work[:, 512 * i:512 * i + 512] for i in range(4)]
        sw_s = [work[:, 2048 + 512 * i:2560 + 512 * i] for i in range(2)]
        hd_s = [work[:, 3072 + 512 * i:3584 + 512 * i] for i in range(2)]
        ident, tri = sb("ident", [P, P]), sb("tri", [P, E, E])
        mask = x2[:, 0, :]
        epst, mhalf, gate = sb("epst", [P, NBLK]), sb("mhalf", [P, NBLK]), sb("gate", [P, 3])
        st, mv, var, rstd = sb("st", [P, NBLK, 6]), sb("mv", [P, NBLK, 2]), sb("var", [P, NBLK]), sb("rstd", [P, NBLK])
        nmx, sums, rsum = sb("nmx", [P, NH]), sb("sums", [P, NH]), sb("rsum", [P, NH])
        lg, mx, dl, ex = sb("lg", [P, NBLK, E]), sb("mx", [P, NBLK]), sb("dl", [P, NBLK, E]), sb("ex", [P, NBLK, E])
        se, s2, den, rden = (sb(n, [P, NBLK]) for n in ("se", "s2", "den", "rden"))
        gt, eq = sb("gt", [P, NBLK, E, E]), sb("eq", [P, NBLK, E, E])
        rank, ew, w = sb("rank", [P, NBLK, E]), sb("ew", [P, NBLK, E]), sb("w", [P, NBLK, E])
        w_t = sb("w_t", [E, GT])

        raw_gu = qt[:, :, :].rearrange("p a b -> p (a b)").rearrange("p (e a m) -> p e a m", e=E, a=2)
        raw_v = vt[:, :, :].rearrange("p a b -> p (a b)")
        raw_qkv = raw_v[:, 1024:4096].rearrange("p (a n) -> p a n", a=3)
        raw_r = raw_v[:, 4096:4608].rearrange("p (q c) -> p q c", q=4)
        raw_rt = raw_v[:, 4608:4616]
        raw_b = kt[:, 0:1, :].rearrange("p a b -> p (a b)")[:, 0:512]
        raw_bias = kt[:, 1:2, :].rearrange("p a b -> p (a b)")[:, 0:128]
        negs = kt[:, 2:4, :].rearrange("p a b -> p (a b)")[:, 0:1024]
        BG, BU, BQ, BP, BR, NBIAS = 0, 16, 32, 40, 41, 45

        pieces = ([(raw_rt, rt_hi[:, :], rt_lo[:, :])]
                  + [(raw_gu[:, e].rearrange("p a m -> p (a m)"), gu_hi[:, e].rearrange("p a m -> p (a m)"),
                      gu_lo[:, e].rearrange("p a m -> p (a m)")) for e in range(E)]
                  + [(raw_r.rearrange("p q c -> p (q c)"), r_hi[:, :, :].rearrange("p q c -> p (q c)"),
                      r_lo[:, :, :].rearrange("p q c -> p (q c)")), (raw_b, b_hi[:, :], b_lo[:, :])]
                  + [(raw_qkv[:, a, n:n + 512], qkv_hi[:, a, n:n + 512], qkv_lo[:, a, n:n + 512])
                     for a in range(3) for n in (0, 512)])
        NPIECE = len(pieces)

        s_x, s_rt, s_bias, s_wo, s_wp, s_bo, s_wr, s_brev, s_neg = (
            sem(n) for n in ("x_loaded", "router_loaded", "bias_loaded", "wo_loaded", "wproj_loaded",
                             "bo_loaded", "wr_loaded", "brev_loaded", "skew_filled"))
        s_gu = [sem(f"gu_loaded{e}") for e in range(E)]
        s_qkv = [sem(f"qkv_loaded{a}") for a in range(3)]
        zeroed, const_ready, negs_ready = sem("zeroed"), sem("const_ready"), sem("negs_ready")
        split_hi, split_lo, kv_zeroed = sem("split_hi"), sem("split_lo"), sem("kv_zeroed")
        bq_scaled = sem("bq_scaled")
        misc_full, misc_done = sem("misc_full"), sem("misc_done")
        stats_done, mv_ready, var_ready, rstd_ready, xn_ready, xh_ready = (
            sem(n) for n in ("stats_done", "mv_ready", "var_ready", "rstd_ready", "xn_ready", "xh_ready"))
        rt_link, ex_ready, wd_stored = sem("rt_link"), sem("ex_ready"), sem("wd_stored")
        g_full, u_full, sg_ready, sw_ready, h_ready, h_used = (
            sem(n) for n in ("gate_full", "up_full", "silu_ready", "weighted_ready", "hidden_ready", "hidden_used"))
        y_full, y_done, x1_done, x3_done, stored = (
            sem(n) for n in ("y_full", "y_done", "x1_done", "x3_done", "stored"))
        qkv_full = [sem(f"qkv_full{i}") for i in range(2)]
        qkv_done = [sem(f"qkv_done{i}") for i in range(2)]
        carried, rs_hi = sem("carried"), sem("rs_hi")
        skew_stored = [sem(f"skew_stored{i}") for i in range(2)]
        wide_full = [sem(f"wide_full{i}") for i in range(4)]
        s_full, l_ready, p_ready, rc_ready, pn_ready, pt_full, pt_done, av_full, av_done, z_full, z_done = (
            sem(n) for n in ("scores_full", "logits_ready", "exp_ready", "recip_ready", "normed_ready",
                             "pt_full", "pt_done", "av_full", "av_done", "z_full", "z_done"))

        RT = 14

        block = ctx.enter_context(nc.Block())

        @block.sync
        def _(sp):
            def wait_all(*waits):
                for _, n in waits:
                    if not isinstance(n, int):
                        sp.compute_val(n)
                for s, n in waits:
                    sp.wait_ge(s, n)

            def load_x(g):
                sp.dma_start(x0[:, :, :], x_in[bass.ds(g * GT, GT), :].rearrange("(t p) d -> p t d", p=P)).then_inc(s_x, 16)

            def store_w(where, g, stage, f, slot):
                sp.wait_ge(misc_done, misc_use(where, g, stage, "w") + 1)
                sp.dma_start(wd[slot].rearrange("(e t) -> e t", e=E), w_t[:, :]).then_inc(wd_stored, 16)

            def spread_w(where, g, f, slot, second):
                for s in range(4):
                    waits = [(wd_stored, (f + 1) * 16)] if s == 0 else []
                    if where != "pro" and not second:
                        waits.append((l_ready, g * NH + 4 * (12 + s) + 4))
                    if second:
                        waits.append((sw_ready, (f - 1) * NCH + 4 * s + 4))
                    wait_all(*waits)
                    src = wd[slot:slot + 1, s * 1024:(s + 1) * 1024].to_broadcast([P, 1024])
                    sp.dma_start(wide[:, s, :], src).then_inc(wide_full[s], 16)

            def store_e(where, g, stage, gq, q):
                waits = [(misc_done, misc_use(where, g, stage, f"e{q}") + 1)]
                if where != "pro":
                    waits.append((wide_full[q % 4], band_uses(gq, q) * 16 - (32 if q < 4 else 0)))
                wait_all(*waits)
                d = skew[q % 4]
                dst = bass.AP(d.tensor, d.offset + 1, [[2 * P + 1, P], [2 * P * P, 4], [1, P]])
                sp.dma_start(dst, es[:, q % 2, :].rearrange("p (h j) -> p h j", h=4)).then_inc(skew_stored[q % 2], 16)

            def load_band(where, g, gq, q):
                f = 0 if where == "pro" else g * 2 + 2
                wait_all((skew_stored[q % 2], gq * (8 * NQ) + 16 * (q // 2 + 1)),
                         (l_ready, gq * NH + 4 * (q - 4) + 4) if q >= 4
                         else (sw_ready, f * NCH + 4 * q + 4))
                sp.dma_start(wide[:, q % 4, :].rearrange("p (h c) -> p h c", h=4),
                             skew[q % 4].rearrange("(h p c) -> p h c", h=4, p=P)).then_inc(wide_full[q % 4], 16)

            def store_x(g):
                sp.wait_ge(x3_done, g + 1)
                sp.dma_start(out[bass.ds(g * GT, GT), :].rearrange("(t p) d -> p t d", p=P), x2[:, :, :]).then_inc(stored, 16)

            load_x(0)
            sp.dma_start(raw_rt, wrt).then_inc(s_rt, 16)
            sp.wait_ge(zeroed, 1)
            sp.dma_start(raw_bias[BG:BU, :], bg.rearrange("e (m p) -> (e m) p", p=P)).then_inc(s_bias, 16)
            sp.dma_start(raw_bias[BU:BQ, :], bu.rearrange("e (m p) -> (e m) p", p=P)).then_inc(s_bias, 16)
            sp.dma_start(raw_bias[BQ:BP, :], bq.rearrange("(a p) -> a p", p=P)).then_inc(s_bias, 16)
            sp.dma_start(raw_bias[BP:BR, :], bproj.rearrange("(a p) -> a p", p=P)).then_inc(s_bias, 16)
            for half in range(2):
                sp.dma_start(raw_bias[BR:NBIAS, 64 * half:64 * half + 40], br.rearrange("(q c) -> q c", q=4)).then_inc(s_bias, 16)
            for e in range(E):
                sp.dma_start(raw_gu[:, e, 0, :], wg[e]).then_inc(s_gu[e], 16)
                sp.dma_start(raw_gu[:, e, 1, :], wu[e]).then_inc(s_gu[e], 16)
                if e == 1:
                    sp.dma_start(bo_s[:, :], bo).then_inc(s_bo, 16)
                    sp.dma_start(wo_s[:, :, :], wo.rearrange("e (m p) d -> p (e m) d", p=P)).then_inc(s_wo, 16)
            store_w("pro", 0, "route", 0, 0)
            spread_w("pro", 0, 0, 0, False)
            sp.wait_ge(zeroed, 3)
            for half in range(2):
                sp.dma_start(raw_r[:, :, 64 * half:64 * half + 40], wr.rearrange("d (q c) -> d q c", q=4)).then_inc(s_wr, 16)
                for h in range(4):
                    sp.dma_start(raw_b[64 * half + NB * h:64 * half + NB * h + NB, P * h:P * h + P], brev).then_inc(s_brev, 16)
            for a, wx in enumerate((wq, wk, wv)):
                sp.dma_start(raw_qkv[:, a, :], wx).then_inc(s_qkv[a], 16)
            sp.dma_start(wp_s[:, :, :], wproj.rearrange("(a p) d -> p a d", p=P)).then_inc(s_wp, 16)
            sp.wait_ge(negs_ready, 1)
            for q in range(4):
                sp.dma_start(skew[q].rearrange("(p c) -> p c", p=P), negs).then_inc(s_neg if q else stored, 16)
            sp.wait_ge(s_neg, 48)
            sp.wait_ge(stored, 16)
            for q in range(4):
                store_e("pro", 0, "qkv", 0, q)
                if q:
                    load_band("pro", 0, 0, q - 1)
            load_band("pro", 0, 0, 3)

            def attention(where, g):
                if where == "loop":
                    sp.wait_ge(x1_done, g + 1)
                    load_x(g + 1)
                for q in range(4, NQ):
                    store_e(where, g, "att", g, q)
                    if q > 4:
                        load_band(where, g, g, q - 1)
                    if q == MISC_W_STEP + 3 and where == "loop":
                        store_w(where, g, "att", g * 2 + 1, 1)
                load_band(where, g, g, NQ - 1)

            with sp.Fori(0, NGROUP - 1) as g:
                attention("loop", g)
                spread_w("loop", g, g * 2 + 1, 1, False)
                store_w("loop", g, "ffn1", g * 2 + 2, 0)
                spread_w("loop", g, g * 2 + 2, 0, True)
                for q in range(4):
                    store_e("loop", g, "qkv", g + 1, q)
                    if q:
                        load_band("loop", g, g + 1, q - 1)
                load_band("loop", g, g + 1, 3)
                store_x(g)
            last = NGROUP - 1
            attention("last", last)
            store_w("last", last, "ffn1", 2 * last + 1, 1)
            spread_w("last", last, 2 * last + 1, 1, False)
            store_x(last)
            sp.wait_ge(stored, 16 + 16 * NGROUP)
            for s in skew_stored:
                sp.wait_ge(s, 8 * NQ * NGROUP)
            sp.wait_ge(wd_stored, 16 * 2 * NGROUP)

        @block.gpsimd
        def _(pool):
            def affine(tile, pattern, base, channel, fill, op):
                return nc.gpsimd.affine_select(out=tile, in_=tile, compare_op=op, fill=fill, base=base,
                                               pattern=pattern, channel_multiplier=channel)

            nc.gpsimd.memset(raw_bias[:, :], 0.0).then_inc(zeroed, 1)
            nc.gpsimd.memset(ident[:, :], 0.0).then_inc(const_ready, 1)
            nc.gpsimd.memset(tri[:, :, :], 1.0).then_inc(const_ready, 1)
            nc.gpsimd.memset(mask, 0.0).then_inc(const_ready, 1)
            nc.gpsimd.memset(epst[:, :], EPS).then_inc(const_ready, 1)
            nc.gpsimd.memset(mhalf[:, :], -0.5).then_inc(const_ready, 1)
            pool.wait_ge(const_ready, 5)
            affine(ident[:, :], [[-1, P]], 0, 1, 1.0, ALU.not_equal).then_inc(const_ready, 1)
            affine(tri[:, :, :], [[1, E], [-1, E]], -1, 0, 0.0, ALU.is_ge).then_inc(const_ready, 1)
            affine(mask, [[1, P]], -(P - 1), 1, NEG, ALU.is_ge).then_inc(const_ready, 1)
            nc.gpsimd.memset(raw_r, 0.0).then_inc(zeroed, 1)
            nc.gpsimd.memset(raw_b, 0.0).then_inc(zeroed, 1)

            def rstd_of(n):
                pool.wait_ge(mv_ready, n + 1)
                nc.gpsimd.tensor_tensor(var[:, :], mv[:, :, 1], epst[:, :], ALU.add).then_inc(var_ready, 1)
                pool.wait_ge(var_ready, n + 1)
                nc.gpsimd.tensor_tensor(rstd[:, :], var[:, :], mhalf[:, :], ALU.pow).then_inc(rstd_ready, 1)

            def ffn(where, g, f, second, hooks):
                for c in range(NCH):
                    for hook in hooks.get(c, []):
                        hook()
                    if c % 4 == 0:
                        pool.wait_ge(wide_full[c // 4], weight_uses(where, g, second) * 16 + 16)
                    if not (where == "pro" and c < 2):
                        pool.wait_ge(h_ready, f * NCH + c - 1)
                    pool.wait_ge(sg_ready, f * NCH + c + 1)
                    wb = wide[:, c // 4, 512 * (c // 2 % 2):512 * (c // 2 % 2) + 512]
                    nc.gpsimd.tensor_tensor(sw_s[c % 2], sg_s[c % 4], wb, ALU.mult).then_inc(sw_ready, 1)

            def attention(where, g):
                for p in range(NP):
                    if p == 4 and where == "loop":
                        rstd_of(g * 3 + 2)
                    if p >= 4:
                        pool.wait_ge(pt_full, g * NP + p - 3)
                    pool.wait_ge(rc_ready, g * NP + p + 1)
                    ri = rsum[:, 2 * p:2 * p + 2].unsqueeze(2).to_broadcast([P, 2, 256])
                    nc.gpsimd.tensor_tensor(pn_s[p % 4].rearrange("p (h c) -> p h c", h=2),
                                            ex_s[p % 4].rearrange("p (h c) -> p h c", h=2),
                                            ri, ALU.mult).then_inc(pn_ready, 1)

            rstd_of(0)
            ffn("pro", 0, 0, False, {})
            nc.gpsimd.memset(negs, NEG).then_inc(negs_ready, 1)
            rstd_of(1)
            pool.wait_ge(split_lo, NPIECE)
            pool.wait_ge(s_neg, 48)
            pool.wait_ge(stored, 16)
            pool.wait_ge(misc_done, 1)
            nc.gpsimd.memset(kt[:, :, 0:P], 0.0).then_inc(kv_zeroed, 1)
            nc.gpsimd.memset(vt[:, 0, :], 0.0).then_inc(kv_zeroed, 1)
            with pool.Fori(0, NGROUP - 1) as g:
                attention("loop", g)
                ffn("loop", g, g * 2 + 1, False, {2: [lambda: rstd_of(g * 3 + 3)]})
                ffn("loop", g, g * 2 + 2, True, {3: [lambda: rstd_of(g * 3 + 4)]})
            last = NGROUP - 1
            attention("last", last)
            rstd_of(3 * last + 2)
            ffn("last", last, 2 * last + 1, False, {})

        @block.scalar
        def _(act):
            def split(i, loaded):
                for s, n in loaded:
                    act.wait_ge(s, n)
                raw, hi, _ = pieces[i]
                nc.scalar.activation(hi, raw, ACT.Copy).then_inc(split_hi, 1)

            def x_hi(where, g, stage, buf):
                act.wait_ge(misc_full, misc_use(where, g, stage, "x") + 1)
                nc.scalar.activation(xh[buf][:, :], misc[:, :], ACT.Copy).then_inc(xh_ready, 1)

            def route_exp(f):
                act.wait_ge(rt_link, f * RT + 3)
                nc.scalar.activation(ex[:, :, :], dl[:, :, :], ACT.Exp).then_inc(ex_ready, 1)

            def w_out(where, g, stage, f):
                if where != "pro":
                    act.wait_ge(wd_stored, f * 16)
                act.wait_ge(misc_full, misc_use(where, g, stage, "w") + 1)
                nc.scalar.activation(w_t[:, :], misc[0:E, :], ACT.Copy).then_inc(misc_done, 1)

            def z_out(g):
                act.wait_ge(z_full, g + 1)
                nc.scalar.activation(yz, acc[:, :], ACT.Identity, bias=bias[:, BP:BP + 1]).then_inc(z_done, 1)

            def ffn(where, f, hooks):
                for c in range(NCH):
                    for hook in hooks.get(c, []):
                        hook()
                    if not (where == "pro" and c < 4):
                        act.wait_ge(sw_ready, f * NCH + c - 3)
                    act.wait_ge(g_full, f * NCH + c + 1)
                    nc.scalar.activation(sg_s[c % 4], bank[c % 2][:, :], ACT.Silu,
                                         bias=bias[:, BG + c:BG + c + 1]).then_inc(sg_ready, 1)
                act.wait_ge(y_full, f + 1)
                nc.scalar.activation(yz, acc[:, :], ACT.Copy, scale=0.5).then_inc(y_done, 1)

            def e_out(where, g, stage, gq, q):
                act.wait_ge(skew_stored[q % 2], gq * (8 * NQ) + 16 * (q // 2))
                act.wait_ge(misc_full, misc_use(where, g, stage, f"e{q}") + 1)
                nc.scalar.activation(es[:, q % 2, :], misc[:, :], ACT.Copy).then_inc(misc_done, 1)

            def qkv(where, g, gq):
                n = 0
                for i in range(NOUT):
                    if i % 4 < 2:
                        act.wait_ge(qkv_full[0], gq * (NOUT // 2) + n + 1)
                        src, n = bank[i % 4][:, :], n + 1
                        if i < 8:
                            nc.scalar.activation(qt[:, i, :], src, ACT.Identity, scale=0.125,
                                                 bias=bias[:, BQ + i:BQ + i + 1]).then_inc(qkv_done[0], 1)
                        elif i < 16:
                            nc.scalar.activation(kt[:, i - 8, P:], src, ACT.Copy).then_inc(qkv_done[0], 1)
                        else:
                            j = i - 16
                            nc.scalar.activation(vt[:, 1 + j // 2, 512 * (j % 2):512 * (j % 2) + 512], src,
                                                 ACT.Copy).then_inc(qkv_done[0], 1)
                    if i in (1, 3, 5, 7):
                        q = i // 2
                        act.wait_ge(misc_full, misc_use(where, g, "qkv", f"r{q}") + 1)
                        nc.scalar.activation(rs[:, q, :], misc[:, :], ACT.Identity,
                                             bias=bias[:, BR + q:BR + q + 1]).then_inc(rs_hi, 1)
                    if i in (12, 15, 18, 21) and where != "pro":
                        e_out(where, g, "qkv", gq, i // 3 - 4)

            def attention(where, g):
                for s in range(NQ + LAG):
                    if s == MISC_X_STEP and where == "loop":
                        x_hi(where, g, "att", 0)
                    if s == MISC_W_STEP and where == "loop":
                        w_out(where, g, "att", g * 2 + 1)
                    if s < NQ:
                        for i in range(4):
                            n = 4 * s + i
                            if i % 2 == 0 and n >= 8:
                                act.wait_ge(pn_ready, g * NP + n // 2 - 3)
                            act.wait_ge(l_ready, g * NH + n + 1)
                            nc.scalar.activation(ex_s[n // 2 % 4][:, 256 * (i % 2):256 * (i % 2) + 256], lg_s[i],
                                                 ACT.Exp, bias=nmx[:, n:n + 1], scale=-1.0,
                                                 accum_out=sums[:, n:n + 1]).then_inc(p_ready, 1)
                    if s + 4 < NQ:
                        e_out(where, g, "att", g, s + 4)
                    if s == MISC_ROUTE_STEP and where == "loop":
                        route_exp(g * 2 + 1)
                    if s >= LAG and (s - LAG) % 2 == 1:
                        u = (s - LAG) // 2
                        act.wait_ge(av_full, g * NP + 4 * u + 4)
                        nc.scalar.activation(qt[:, 4 * (u % 2):4 * (u % 2) + 4, P * (u // 2):P * (u // 2) + P],
                                             acc[:, :].rearrange("p (a t) -> p a t", a=4),
                                             ACT.Copy).then_inc(av_done, 1)
                z_out(g)

            act.wait_ge(misc_full, 1)
            nc.scalar.activation(bias[:, 0:NBIAS], misc[:, 0:NBIAS], ACT.Copy).then_inc(misc_done, 1)
            split(0, [(s_rt, 16)])
            x_hi("pro", 0, "route", 0)
            split(1, [(s_gu[0], 32)])
            route_exp(0)
            split(2, [(s_gu[1], 32)])
            w_out("pro", 0, "route", 0)
            loads = ([[(s_gu[e], 32)] for e in range(2, E)] + [[(s_wr, 32)], [(s_brev, 128)]]
                     + [[(s_qkv[a], 16)] for a in range(3) for _ in range(2)])
            ffn("pro", 0, {c: [lambda c=c: split(3 + c, loads[c])] for c in range(len(loads))})
            x_hi("pro", 0, "ffn2", 0)
            act.wait_ge(kv_zeroed, 2)
            act.wait_ge(bq_scaled, 1)
            qkv("pro", 0, 0)
            with act.Fori(0, NGROUP - 1) as g:
                attention("loop", g)

                def carry():
                    nc.scalar.activation(kt[:, :, 0:P], kt[:, :, GT:GT + P], ACT.Copy).then_inc(carried, 1)
                    nc.scalar.activation(vt[:, 0, :], vt[:, NBLK, :], ACT.Copy).then_inc(carried, 1)

                ffn("loop", g * 2 + 1, {1: [carry], 3: [lambda: x_hi("loop", g, "ffn1", 1)],
                                        6: [lambda: route_exp(g * 2 + 2)],
                                        9: [lambda: w_out("loop", g, "ffn1", g * 2 + 2)]})
                ffn("loop", g * 2 + 2, {5: [lambda: x_hi("loop", g, "ffn2", 0)]})
                act.wait_ge(carried, g * 2 + 2)
                qkv("loop", g, g + 1)
            last = NGROUP - 1
            attention("last", last)
            x_hi("last", last, "ffn1", 1)
            route_exp(2 * last + 1)
            w_out("last", last, "ffn1", 2 * last + 1)
            ffn("last", 2 * last + 1, {})

        @block.vector
        def _(dve):
            v = nc.vector

            def split(i):
                dve.wait_ge(split_hi, i + 1)
                raw, hi, lo = pieces[i]
                v.tensor_tensor(lo, raw, hi.bitcast(F32), ALU.subtract).then_inc(split_lo, 1)

            def stats(n, x):
                for t in range(NBLK):
                    ins = v.bn_stats(st[:, t, :], x[:, t, :])
                ins.then_inc(stats_done, 1)
                dve.wait_ge(stats_done, n + 1)
                v.memset(gate[:, 2:3], 0.0)
                for t in range(NBLK):
                    ins = v.bn_aggr(mv[:, t, :], st[:, t, :])
                ins.then_inc(mv_ready, 1)

            def normalise(n, x):
                dve.wait_ge(rstd_ready, n + 1)
                for t in range(NBLK):
                    ins = v.tensor_scalar(xn[:, t, :], x[:, t, :], mv[:, t, 0:1], rstd[:, t:t + 1],
                                          ALU.subtract, ALU.mult)
                ins.then_inc(xn_ready, 1)

            def x_lo(where, g, stage, n, buf):
                dve.wait_ge(xh_ready, n + 1)
                v.tensor_tensor(xl[buf][:, :], misc[:, :], xh[buf][:, :].bitcast(F32), ALU.subtract).then_inc(misc_done, 1)

            def residual(where, g, stage, use, new, old):
                dve.wait_ge(misc_full, misc_use(where, g, stage, use) + 1)
                v.tensor_tensor(new[:, :, :], misc[:, :].rearrange("p (t d) -> p t d", t=NBLK), old[:, :, :],
                                ALU.add).then_inc(misc_done, 1)
                dve.wait_ge(misc_done, misc_use(where, g, stage, use) + 1)

            def per_token(t):
                return t[:, :].unsqueeze(2).to_broadcast([P, NBLK, E])

            def route_a(where, g, stage, f):
                dve.wait_ge(misc_full, misc_use(where, g, stage, "route") + 1)
                v.tensor_copy(lg[:, :, :], misc[:, 0:NBLK * E].rearrange("p (t e) -> p t e", t=NBLK)).then_inc(misc_done, 1)
                dve.wait_ge(misc_done, misc_use(where, g, stage, "route") + 1)
                v.tensor_reduce(mx[:, :], lg[:, :, :], X, ALU.max).then_inc(rt_link, 1)
                dve.wait_ge(rt_link, f * RT + 1)
                v.tensor_tensor(dl[:, :, :], lg[:, :, :], per_token(mx), ALU.subtract).then_inc(rt_link, 2)

            def route_b(f):
                n = [3]

                def link(ins):
                    n[0] += 1
                    ins.then_inc(rt_link, 1)
                    dve.wait_ge(rt_link, f * RT + n[0])

                other = ex[:, :, :].unsqueeze(2).to_broadcast([P, NBLK, E, E])
                own = ex[:, :, :].unsqueeze(3).to_broadcast([P, NBLK, E, E])
                dve.wait_ge(ex_ready, f + 1)
                link(v.tensor_reduce(se[:, :], ex[:, :, :], X, ALU.add))
                link(v.tensor_tensor(gt[:, :, :, :], other, own, ALU.is_gt))
                link(v.tensor_tensor(eq[:, :, :, :], other, own, ALU.is_equal))
                link(v.tensor_tensor(eq[:, :, :, :], eq[:, :, :, :],
                                     tri[:, :, :].unsqueeze(1).to_broadcast([P, NBLK, E, E]), ALU.mult))
                link(v.tensor_tensor(gt[:, :, :, :], gt[:, :, :, :], eq[:, :, :, :], ALU.add))
                link(v.tensor_reduce(rank[:, :, :], gt[:, :, :, :], X, ALU.add))
                link(v.scalar_tensor_tensor(ew[:, :, :], rank[:, :, :], 1.5, ex[:, :, :], ALU.is_lt, ALU.mult))
                link(v.tensor_reduce(s2[:, :], ew[:, :, :], X, ALU.add))
                link(v.scalar_tensor_tensor(den[:, :], se[:, :], 1.0e-8, s2[:, :], ALU.mult, ALU.add))
                link(v.reciprocal(rden[:, :], den[:, :]))
                v.tensor_tensor(w[:, :, :], ew[:, :, :], per_token(rden), ALU.mult).then_inc(rt_link, 1)
                assert n[0] + 1 == RT

            def ffn(where, f, hooks):
                for c in range(NCH):
                    for hook in hooks.get(c, []):
                        hook()
                    if c >= 2:
                        dve.wait_ge(h_used, f * (NCH - 1) + c - 1)
                    dve.wait_ge(u_full, f * NCH + c + 1)
                    dve.wait_ge(sw_ready, f * NCH + c + 1)
                    v.scalar_tensor_tensor(hd_s[c % 2], bank[2 + c % 2][:, :], bias[:, BU + c:BU + c + 1],
                                           sw_s[c % 2], ALU.add, ALU.mult).then_inc(h_ready, 1)

            def qkv(where, g, gq):
                n = 0
                for i in range(NOUT):
                    if i % 4 >= 2:
                        dve.wait_ge(qkv_full[1], gq * (NOUT // 2) + n + 1)
                        src, n = bank[i % 4][:, :], n + 1
                        if i < 8:
                            v.tensor_scalar(qt[:, i, :], src, 0.125, bias[:, BQ + i:BQ + i + 1],
                                            ALU.mult, ALU.add).then_inc(qkv_done[1], 1)
                        elif i < 16:
                            v.tensor_copy(kt[:, i - 8, P:], src).then_inc(qkv_done[1], 1)
                        else:
                            j = i - 16
                            v.tensor_copy(vt[:, 1 + j // 2, 512 * (j % 2):512 * (j % 2) + 512], src).then_inc(qkv_done[1], 1)
                    if i in (1, 3, 5, 7):
                        q = i // 2
                        dve.wait_ge(rs_hi, gq * 4 + q + 1)
                        v.scalar_tensor_tensor(rs[64:P, q, :], misc[64:P, :], bias[64:P, BR + q:BR + q + 1],
                                               rs[64:P, q, :].bitcast(F32), ALU.add, ALU.subtract).then_inc(misc_done, 1)
                    if i == 9 and where == "loop":
                        dve.wait_ge(stored, g * 16)  if False else None
                        residual(where, g, "qkv", "y", x2, x2)
                        v.memset(gate[:, 1:2], 0.0).then_inc(x3_done, 1)
                    if i in (12, 15, 18, 21) and where == "pro":
                        q = i // 3 - 4
                        if q >= 2:
                            dve.wait_ge(skew_stored[q % 2], 16 * (q // 2))
                        dve.wait_ge(misc_full, misc_use(where, g, "qkv", f"e{q}") + 1)
                        v.tensor_tensor(es[:, q % 2, :].rearrange("p (h j) -> p h j", h=4),
                                        misc[:, :].rearrange("p (h j) -> p h j", h=4),
                                        mask.unsqueeze(1).to_broadcast([P, 4, P]), ALU.add).then_inc(misc_done, 1)

            def pt_out(g, p):
                if p >= 2:
                    dve.wait_ge(av_full, g * NP + p - 1)
                dve.wait_ge(pt_full, g * NP + p + 1)
                v.tensor_copy(pt_s[p % 2], ptb[p % 2][:, :]).then_inc(pt_done, 1)

            def recip(g, p):
                dve.wait_ge(p_ready, g * NH + 2 * p + 2)
                v.reciprocal(rsum[:, 2 * p:2 * p + 2], sums[:, 2 * p:2 * p + 2]).then_inc(rc_ready, 1)

            def attention(where, g):
                for s in range(NQ + LAG):
                    if s >= LAG:
                        pt_out(g, 2 * (s - LAG))
                    if 1 <= s <= NQ:
                        recip(g, 2 * s - 1)
                    if s >= LAG:
                        pt_out(g, 2 * (s - LAG) + 1)
                    if where == "loop":
                        if s == 1:
                            dve.wait_ge(s_x, g * 16 + 32)
                            stats(g * 3 + 2, x0)
                        if s == 3:
                            normalise(g * 3 + 2, x0)
                        if s == MISC_X_STEP:
                            x_lo(where, g, "att", g * 3 + 2, 0)
                        if s == MISC_ROUTE_STEP:
                            route_a(where, g, "att", g * 2 + 1)
                        if s == MISC_ROUTE_STEP + 2:
                            route_b(g * 2 + 1)
                    if s < NQ:
                        dve.wait_ge(s_full, g * NQ + s + 1)
                        dve.wait_ge(wide_full[s % 4], band_uses(g, s) * 16 + 16)
                        if s:
                            dve.wait_ge(p_ready, g * NH + 4 * s)
                        v.memset(gate[:, 0:1], 0.0)
                        for i in range(4):
                            n = 4 * s + i
                            v.tensor_tensor_reduce(out=lg_s[i],
                                                   in0=bank[2 * (s % 2) + i % 2][:, 256 * (i // 2):256 * (i // 2) + 256],
                                                   in1=wide[:, s % 4, 256 * i:256 * i + 256],
                                                   scale=-1.0, scalar=3.0e38, op0=ALU.add, op1=ALU.min,
                                                   accum_out=nmx[:, n:n + 1]).then_inc(l_ready, 1)
                        recip(g, 2 * s)

            dve.wait_ge(s_x, 16)
            stats(0, x0)
            normalise(0, x0)
            split(0)
            dve.wait_ge(misc_done, 1)
            v.tensor_scalar(bias[:, BQ:BP], bias[:, BQ:BP], 0.125, None, ALU.mult).then_inc(bq_scaled, 1)
            x_lo("pro", 0, "route", 0, 0)
            split(1)
            route_a("pro", 0, "route", 0)
            route_b(0)
            split(2)
            ffn("pro", 0, {c: [lambda c=c: split(3 + c)] for c in range(NPIECE - 3)})
            residual("pro", 0, "ffn2", "y", x1, x0)
            v.memset(gate[:, 1:2], 0.0).then_inc(x1_done, 1)
            stats(1, x1)
            normalise(1, x1)
            x_lo("pro", 0, "ffn2", 1, 0)
            dve.wait_ge(kv_zeroed, 2)
            dve.wait_ge(bq_scaled, 1)
            qkv("pro", 0, 0)
            with dve.Fori(0, NGROUP - 1) as g:
                attention("loop", g)

                def tail2():
                    dve.wait_ge(stored, g * 16 + 16)
                    residual("loop", g, "ffn1", "z", x2, x1)
                    stats(g * 3 + 3, x2)

                def tail1():
                    residual("loop", g, "ffn2", "y", x1, x0)
                    v.memset(gate[:, 1:2], 0.0).then_inc(x1_done, 1)
                    stats(g * 3 + 4, x1)

                ffn("loop", g * 2 + 1, {1: [tail2], 2: [lambda: normalise(g * 3 + 3, x2)],
                                        3: [lambda: x_lo("loop", g, "ffn1", g * 3 + 3, 1)],
                                        5: [lambda: route_a("loop", g, "ffn1", g * 2 + 2)],
                                        7: [lambda: route_b(g * 2 + 2)]})
                ffn("loop", g * 2 + 2, {2: [tail1], 4: [lambda: normalise(g * 3 + 4, x1)],
                                        5: [lambda: x_lo("loop", g, "ffn2", g * 3 + 4, 0)]})
                dve.wait_ge(carried, g * 2 + 2)
                qkv("loop", g, g + 1)
            last = NGROUP - 1
            attention("last", last)
            dve.wait_ge(stored, last * 16 + 16)
            residual("last", last, "ffn1", "z", x2, x1)
            stats(3 * last + 2, x2)
            normalise(3 * last + 2, x2)
            x_lo("last", last, "ffn1", 3 * last + 2, 1)
            route_a("last", last, "ffn1", 2 * last + 1)
            route_b(2 * last + 1)
            ffn("last", 2 * last + 1, {})
            residual("last", last, "end", "y", x2, x2)
            v.memset(gate[:, 1:2], 0.0).then_inc(x3_done, 1)

        @block.tensor
        def _(pe):
            mm = nc.tensor.matmul

            def three(out_ap, w_hi, w_lo, m_hi, m_lo):
                mm(out_ap, w_hi, m_hi, start=True, stop=False)
                mm(out_ap, w_lo, m_hi, start=False, stop=False)
                return mm(out_ap, w_hi, m_lo, start=False, stop=True)

            def claim(where, g, stage, use):
                n = misc_use(where, g, stage, use)
                if not (where == "pro" and n == 0):
                    pe.wait_ge(misc_done, n)

            def turn(src):
                for t in range(NBLK):
                    ins = nc.tensor.transpose(misc[:, P * t:P * t + P], src(t), ident[:, :])
                ins.then_inc(misc_full, 1)

            def x_turn(where, g, stage, n):
                claim(where, g, stage, "x")
                pe.wait_ge(xn_ready, n + 1)
                turn(lambda t: xn[:, t, :])

            def back(where, g, stage, use, s, count):
                claim(where, g, stage, use)
                pe.wait_ge(s, count)
                turn(lambda t: yz[:, P * t:P * t + P])

            def route(where, g, stage, buf):
                claim(where, g, stage, "route")
                for t in range(NBLK):
                    xt = slice(P * t, P * t + P)
                    o = misc[:, E * t:E * t + E]
                    mm(o, xh[buf][:, xt], rt_hi[:, :], start=True, stop=False)
                    mm(o, xl[buf][:, xt], rt_hi[:, :], start=False, stop=False)
                    ins = mm(o, xh[buf][:, xt], rt_lo[:, :], start=False, stop=True)
                ins.then_inc(misc_full, 1)

            def w_turn(where, g, stage, f):
                claim(where, g, stage, "w")
                pe.wait_ge(rt_link, f * RT + RT)
                for t in range(NBLK):
                    ins = nc.tensor.transpose(misc[0:E, P * t:P * t + P], w[:, t, :], ident[:, :])
                ins.then_inc(misc_full, 1)

            def ffn(where, f, buf, x_use, w_use, acc_free, hooks):
                for c in range(NCH + 2):
                    for hook in hooks.get(c, []):
                        hook()
                    if c < NCH:
                        e, m = c // 2, P * (c % 2)
                        if c == 0:
                            pe.wait_ge(misc_done, x_use + 1)
                        if where == "pro" and c % 2 == 0:
                            pe.wait_ge(split_lo, 2 + e)
                        if not (where == "pro" and c < 2):
                            pe.wait_ge(sg_ready, f * NCH + c - 1)
                        three(bank[c % 2][:, :], gu_hi[:, e, 0, m:m + P], gu_lo[:, e, 0, m:m + P],
                              xh[buf][:, :], xl[buf][:, :]).then_inc(g_full, 1)
                        if not (where == "pro" and c < 2):
                            pe.wait_ge(h_ready, f * NCH + c - 1)
                        three(bank[2 + c % 2][:, :], gu_hi[:, e, 1, m:m + P], gu_lo[:, e, 1, m:m + P],
                              xh[buf][:, :], xl[buf][:, :]).then_inc(u_full, 1)
                    if c == 1:
                        pe.wait_ge(misc_done, w_use + 1)
                        if acc_free:
                            pe.wait_ge(*acc_free)
                        if where == "pro":
                            pe.wait_ge(s_bo, 16)
                            pe.wait_ge(s_wo, 16)
                        mm(acc[:, :], bo_s[:, :], w_t[:, :], start=True, stop=False)
                    if c >= 2:
                        pe.wait_ge(h_ready, f * NCH + c - 1)
                        ins = mm(acc[:, :], wo_s[:, c - 2, :], hd_s[c % 2], start=False, stop=(c == NCH + 1))
                        ins.then_inc(y_full if c == NCH + 1 else h_used, 1)

            def e_mm(where, g, stage, q):
                claim(where, g, stage, f"e{q}")
                blk = slice(P * (q // 4), P * (q // 4) + P)
                mm(misc[:, :], rs[:, q % 4, blk], b_hi[:, :], start=True, stop=False)
                mm(misc[:, :], rs[:, q % 4, blk], b_lo[:, :], start=False, stop=True).then_inc(misc_full, 1)

            def qkv(where, g, gq, f):
                n = [0, 0]
                for i in range(NOUT):
                    side = i % 4 // 2
                    if where == "pro" and i in (0, 8, 16):
                        pe.wait_ge(split_lo, NPIECE)
                    if i >= 4:
                        pe.wait_ge(qkv_done[side], gq * (NOUT // 2) + n[side] - 1)
                    if i < 16:
                        a, c = i // 8, P * (i % 8)
                        ins = three(bank[i % 4][:, :], qkv_hi[:, a, c:c + P], qkv_lo[:, a, c:c + P], xh[0][:, :], xl[0][:, :])
                    else:
                        t, c = P * ((i - 16) // 2), 512 * (i % 2)
                        ins = three(bank[i % 4][:, :], xh[0][:, t:t + P], xl[0][:, t:t + P],
                                    qkv_hi[:, 2, c:c + 512], qkv_lo[:, 2, c:c + 512])
                    ins.then_inc(qkv_full[side], 1)
                    n[side] += 1
                    if i in (0, 2, 4, 6):
                        q = i // 2
                        claim(where, g, "qkv", f"r{q}")
                        three(misc[:, :], r_hi[:, q, :], r_lo[:, q, :], xh[0][:, :], xl[0][:, :]).then_inc(misc_full, 1)
                    if i == 8 and where == "loop":
                        back(where, g, "qkv", "y", y_done, f + 1)
                    if i in (11, 14, 17, 20):
                        e_mm(where, g, "qkv", i // 3 - 3)

            def scores(g, s):
                b = s // 4
                if s >= 2:
                    pe.wait_ge(l_ready, g * NH + 4 * (s - 1))
                for jj in range(2):
                    j = 2 * (s % 4) + jj
                    for hh in range(2):
                        r = slice(64 * hh, 64 * hh + 64)
                        ins = mm(bank[2 * (s % 2) + hh][:, 256 * jj:256 * jj + 256], qt[r, j, P * b:P * b + P],
                                 kt[r, j, P * b:P * b + 2 * P], start=True, stop=True)
                ins.then_inc(s_full, 1)

            def pt(g, p):
                pe.wait_ge(pn_ready, g * NP + p + 1)
                if p >= 2:
                    pe.wait_ge(pt_done, g * NP + p - 1)
                for k in range(4):
                    ins = nc.tensor.transpose(ptb[p % 2][:, P * k:P * k + P], pn_s[p % 4][:, P * k:P * k + P], ident[:, :])
                ins.then_inc(pt_full, 1)

            def av(g, p):
                b, j = p // 8, p % 8
                if p % 4 == 0 and p:
                    pe.wait_ge(av_done, g * (NP // 4) + p // 4)
                if p == 0:
                    pe.wait_ge(y_done, g * 2 + 1)
                pe.wait_ge(pt_done, g * NP + p + 1)
                for k in range(2):
                    for hh in range(2):
                        ins = mm(acc[64 * hh:64 * hh + 64, P * (p % 4):P * (p % 4) + P],
                                 vt[:, b + k, P * j + 64 * hh:P * j + 64 * hh + 64],
                                 pt_s[p % 2][:, 256 * hh + P * k:256 * hh + P * k + P], start=(k == 0), stop=(k == 1))
                ins.then_inc(av_full, 1)

            def attention(where, g):
                for side in range(2):
                    pe.wait_ge(qkv_done[side], (g + 1) * (NOUT // 2))
                for s in range(NQ + LAG):
                    p0 = 2 * (s - LAG)
                    if where == "loop":
                        if s == MISC_X_STEP:
                            x_turn(where, g, "att", g * 3 + 2)
                        if s == MISC_ROUTE_STEP:
                            route(where, g, "att", 0)
                        if s == MISC_W_STEP:
                            w_turn(where, g, "att", g * 2 + 1)
                    if s >= LAG:
                        pt(g, p0)
                        pt(g, p0 + 1)
                    if s < NQ:
                        scores(g, s)
                    if s >= LAG:
                        av(g, p0)
                    if s + 4 < NQ:
                        e_mm(where, g, "att", s + 4)
                    if s >= LAG:
                        av(g, p0 + 1)
                pe.wait_ge(av_done, (g + 1) * (NP // 4))
                for j in range(NPAIR):
                    ins = mm(acc[:, :], wp_s[:, j, :], qt[:, j, :], start=(j == 0), stop=(j == NPAIR - 1))
                ins.then_inc(z_full, 1)

            pe.wait_ge(const_ready, 8)
            pe.wait_ge(s_bias, 96)
            nc.tensor.transpose(misc[:, 0:NBIAS], raw_bias[0:NBIAS, :], ident[0:NBIAS, 0:NBIAS]).then_inc(misc_full, 1)
            x_turn("pro", 0, "route", 0)
            pe.wait_ge(split_lo, 1)
            route("pro", 0, "route", 0)
            w_turn("pro", 0, "route", 0)
            ffn("pro", 0, 0, misc_use("pro", 0, "route", "x"), misc_use("pro", 0, "route", "w"), None, {})
            back("pro", 0, "ffn2", "y", y_done, 1)
            x_turn("pro", 0, "ffn2", 1)
            pe.wait_ge(misc_done, misc_use("pro", 0, "ffn2", "x") + 1)
            pe.wait_ge(s_wp, 16)
            qkv("pro", 0, 0, 0)
            with pe.Fori(0, NGROUP - 1) as g:
                attention("loop", g)
                ffn("loop", g * 2 + 1, 0, misc_use("loop", g, "att", "x"), misc_use("loop", g, "att", "w"),
                    (z_done, g + 1),
                    {1: [lambda: back("loop", g, "ffn1", "z", z_done, g + 1)],
                     3: [lambda: x_turn("loop", g, "ffn1", g * 3 + 3)],
                     5: [lambda: route("loop", g, "ffn1", 1)],
                     9: [lambda: w_turn("loop", g, "ffn1", g * 2 + 2)]})
                ffn("loop", g * 2 + 2, 1, misc_use("loop", g, "ffn1", "x"), misc_use("loop", g, "ffn1", "w"),
                    (y_done, g * 2 + 2),
                    {2: [lambda: back("loop", g, "ffn2", "y", y_done, g * 2 + 2)],
                     5: [lambda: x_turn("loop", g, "ffn2", g * 3 + 4)]})
                pe.wait_ge(misc_done, misc_use("loop", g, "ffn2", "x") + 1)
                qkv("loop", g, g + 1, g * 2 + 2)
            last = NGROUP - 1
            attention("last", last)
            back("last", last, "ffn1", "z", z_done, last + 1)
            x_turn("last", last, "ffn1", 3 * last + 2)
            route("last", last, "ffn1", 1)
            w_turn("last", last, "ffn1", 2 * last + 1)
            ffn("last", 2 * last + 1, 1, misc_use("last", last, "ffn1", "x"), misc_use("last", last, "ffn1", "w"),
                (z_done, last + 1), {})
            back("last", last, "end", "y", y_done, 2 * last + 2)


_INS = ["L0_attn_X", "L0_attn_Wq", "L0_attn_bq", "L0_attn_Wk", "L0_attn_Wv", "L0_attn_Wproj", "L0_attn_bproj",
        "L0_attn_Wr", "L0_attn_br", "L0_attn_b_nd", "L0_ffn_W_router", "L0_ffn_W_gate", "L0_ffn_b_gate",
        "L0_ffn_W_up", "L0_ffn_b_up", "L0_ffn_W_out", "L0_ffn_b_out"]


def kernel(**inputs):
    import numpy as _np
    import concourse.bacc as _bacc
    from concourse import mybir as _mybir
    from concourse.bass_utils import run_bass_kernel_spmd as _run

    nc = _bacc.Bacc("TRN2", target_bir_lowering=False, num_devices=1)
    arrays, args = {}, []
    for name in _INS:
        a = _np.asarray(inputs[name])
        if name == "L0_attn_X":
            a = a.reshape(T, D)
        if name == "L0_attn_b_nd":
            a = a[:, ::-1]
        a = _np.ascontiguousarray(a)
        arrays[f"in_{name}"] = a
        args.append(nc.dram_tensor(f"in_{name}", a.shape, _mybir.dt.from_np(a.dtype), kind="ExternalInput").ap())
    args.append(nc.dram_tensor("out_0", (T, D), _mybir.dt.float32, kind="ExternalOutput").ap())
    macaron(nc, *args)
    r = _run(nc, [arrays], core_ids=[0])
    return r.results[0]["out_0"].reshape(1, T, D)
```

```python
from contextlib import ExitStack

import concourse.bass as bass
from concourse import mybir

ALU = mybir.AluOpType
ACT = mybir.ActivationFunctionType
F32 = mybir.dt.float32
F32R = mybir.dt.float32r
X = mybir.AxisListType.X

P = 128
T, D = 2048, 128
GT = 512
NGROUP = T // GT
NBLK = GT // P
E, M = 8, 256
NCH = E * M // P
H, DQ, NB = 16, 64, 10
NPAIR = H // 2
NQ = 4 * NBLK
NP = 2 * NQ
NH = 4 * NQ
NQK = 16
NV = 8
E_AFTER = (8, 10, 12, 14)
LAG = 2
NEG = -1.0e9
EPS = 1.0e-5

USES_SETUP = ["bias"]
USES_ROUTE = ["x", "route", "w"]
USES_TAIL1 = ["y", "x"]
USES_TAIL2 = ["z", "x", "route", "w"]
USES_ATT_LAST = [f"e{q}" for q in range(4, NQ)]
USES_ATT = ["e4", "e5", "e6", "e7", "x", "e8", "e9", "route", "e10", "e11", "e12", "e13", "e14", "w", "e15"]
USES_QKV0 = ["e0", "e1", "e2", "e3"]
USES_QKV = ["y"] + USES_QKV0
ORDER_PROLOGUE = [("setup", USES_SETUP), ("route", USES_ROUTE), ("ffn2", USES_TAIL1), ("qkv", USES_QKV0)]
ORDER_LOOP = [("att", USES_ATT), ("ffn1", USES_TAIL2), ("ffn2", USES_TAIL1), ("qkv", USES_QKV)]
ORDER_LAST = [("att", USES_ATT_LAST), ("ffn1", USES_TAIL2), ("end", ["y"])]
N_PROLOGUE = sum(len(u) for _, u in ORDER_PROLOGUE)
N_LOOP = sum(len(u) for _, u in ORDER_LOOP)
X_STEP, ROUTE_STEP, W_STEP = 3, 5, 10


def misc_use(where, g, stage, use):
    order, base = {"pro": (ORDER_PROLOGUE, 0), "loop": (ORDER_LOOP, g * N_LOOP + N_PROLOGUE),
                   "last": (ORDER_LAST, (NGROUP - 1) * N_LOOP + N_PROLOGUE)}[where]
    for name, uses in order:
        if name == stage:
            return base + uses.index(use)
        base = base + len(uses)
    raise KeyError(stage)


def band_uses(g, q):
    return g * 6 + (1 if q < 4 else 1 + q // 4)


def weight_uses(where, g, second):
    return 0 if where == "pro" else g * 6 + 5 + (1 if second and where == "loop" else 0)


def macaron(nc, x_in, wq, bq, wk, wv, wproj, bproj, wr, br, brev, wrt, wg, bg, wu, bu, wo, bo, out):
    with ExitStack() as ctx:
        def sb(name, shape, dt=F32):
            return ctx.enter_context(nc.sbuf_tensor(name, shape, dt))

        def sem(name):
            return ctx.enter_context(nc.semaphore(name))

        skew = nc.dram_tensor("skew", (4, 4 * P * 2 * P), F32, kind="Internal").ap()
        wd = nc.dram_tensor("wd", (2, E * GT), F32, kind="Internal").ap()

        bank = [ctx.enter_context(nc.psum_tensor(f"bank{i}", [P, 512], F32)) for i in range(8)]
        acc, misc, ptb = bank[4], bank[5], bank[6:8]
        up_bank = [bank[2], bank[3], bank[6], bank[7]]

        gu_hi, gu_lo = sb("gu_hi", [P, E, 2, M], F32R), sb("gu_lo", [P, E, 2, M], F32R)
        qkv_hi, qkv_lo = sb("qkv_hi", [P, 3, H * DQ], F32R), sb("qkv_lo", [P, 3, H * DQ], F32R)
        r_hi, r_lo = sb("r_hi", [P, 4, P], F32R), sb("r_lo", [P, 4, P], F32R)
        rt_hi, rt_lo = sb("rt_hi", [P, E], F32R), sb("rt_lo", [P, E], F32R)
        b_hi, b_lo = sb("b_hi", [P, 4 * P], F32R), sb("b_lo", [P, 4 * P], F32R)
        wo_s, wp_s, bo_s = sb("wo_s", [P, NCH, D]), sb("wp_s", [P, NPAIR, D]), sb("bo_s", [E, D])
        bias = sb("bias", [P, 48])
        x0, x1, x2 = (sb(f"x{i}", [P, NBLK, D]) for i in range(3))
        xn = sb("xn", [P, NBLK, D])
        xh = [sb("xh_a", [P, GT], F32R), sb("xh_b", [P, GT], F32R)]
        xl = [sb("xl_a", [P, GT], F32R), sb("xl_b", [P, GT], F32R)]
        yz = xn[:, :, :].rearrange("p t d -> p (t d)")
        qt, kt, vt = sb("qt", [P, NPAIR, GT]), sb("kt", [P, NPAIR, GT + P]), sb("vt", [P, NBLK + 1, H * DQ])
        rs = sb("rs", [P, 4, GT], F32R)
        es = sb("es", [P, 2, 4 * P])
        wide = sb("wide", [P, 4, 4 * 2 * P])
        work = sb("work", [P, 6144])
        lg_s = [work[:, 256 * i:256 * i + 256] for i in range(4)]
        ex_s = [work[:, 1024 + 512 * i:1536 + 512 * i] for i in range(4)]
        pn_s = [work[:, 3072 + 512 * i:3584 + 512 * i] for i in range(4)]
        pt_s = [work[:, 5120 + 512 * i:5632 + 512 * i] for i in range(2)]
        sg_s = [work[:, 512 * i:512 * i + 512] for i in range(4)]
        sw_s = [work[:, 2048 + 512 * i:2560 + 512 * i] for i in range(4)]
        hd_s = [work[:, 4096 + 512 * i:4608 + 512 * i] for i in range(4)]
        ident, tri = sb("ident", [P, P]), sb("tri", [P, E, E])
        mask = x2[:, 0, :]
        epst, mhalf, gate = sb("epst", [P, NBLK]), sb("mhalf", [P, NBLK]), sb("gate", [P, 3])
        st, mv, var, rstd = sb("st", [P, NBLK, 6]), sb("mv", [P, NBLK, 2]), sb("var", [P, NBLK]), sb("rstd", [P, NBLK])
        nmx, sums, rsum = sb("nmx", [P, NH]), sb("sums", [P, NH]), sb("rsum", [P, NH])
        lg, mx, dl, ex = sb("lg", [P, NBLK, E]), sb("mx", [P, NBLK]), sb("dl", [P, NBLK, E]), sb("ex", [P, NBLK, E])
        se, s2, den, rden = (sb(n, [P, NBLK]) for n in ("se", "s2", "den", "rden"))
        gt, eq = sb("gt", [P, NBLK, E, E]), sb("eq", [P, NBLK, E, E])
        rank, ew, w = sb("rank", [P, NBLK, E]), sb("ew", [P, NBLK, E]), sb("w", [P, NBLK, E])
        w_t = sb("w_t", [E, GT])

        raw_gu = qt[:, :, :].rearrange("p a b -> p (a b)").rearrange("p (e a m) -> p e a m", e=E, a=2)
        raw_v = vt[:, :, :].rearrange("p a b -> p (a b)")
        raw_qkv = raw_v[:, 1024:4096].rearrange("p (a n) -> p a n", a=3)
        raw_r = raw_v[:, 4096:4608].rearrange("p (q c) -> p q c", q=4)
        raw_rt = raw_v[:, 4608:4616]
        raw_b = kt[:, 0:1, :].rearrange("p a b -> p (a b)")[:, 0:512]
        raw_bias = kt[:, 1:2, :].rearrange("p a b -> p (a b)")[:, 0:128]
        negs = kt[:, 2:4, :].rearrange("p a b -> p (a b)")[:, 0:1024]
        BG, BU, BQ, BP, BR, NBIAS = 0, 16, 32, 40, 41, 45

        pieces = ([(raw_rt, rt_hi[:, :], rt_lo[:, :])]
                  + [(raw_gu[:, e].rearrange("p a m -> p (a m)"), gu_hi[:, e].rearrange("p a m -> p (a m)"),
                      gu_lo[:, e].rearrange("p a m -> p (a m)")) for e in range(E)]
                  + [(raw_r.rearrange("p q c -> p (q c)"), r_hi[:, :, :].rearrange("p q c -> p (q c)"),
                      r_lo[:, :, :].rearrange("p q c -> p (q c)")), (raw_b, b_hi[:, :], b_lo[:, :])]
                  + [(raw_qkv[:, a, n:n + 512], qkv_hi[:, a, n:n + 512], qkv_lo[:, a, n:n + 512])
                     for a in range(3) for n in (0, 512)])
        NPIECE = len(pieces)

        s_x, s_rt, s_bias, s_wo, s_wp, s_bo, s_wr, s_brev, s_neg = (
            sem(n) for n in ("x_loaded", "router_loaded", "bias_loaded", "wo_loaded", "wproj_loaded",
                             "bo_loaded", "wr_loaded", "brev_loaded", "skew_filled"))
        s_gu = [sem(f"gu_loaded{e}") for e in range(E)]
        s_qkv = [sem(f"qkv_loaded{a}") for a in range(3)]
        zeroed, const_ready, negs_ready = sem("zeroed"), sem("const_ready"), sem("negs_ready")
        split_hi, split_lo, kv_zeroed = sem("split_hi"), sem("split_lo"), sem("kv_zeroed")
        bq_scaled = sem("bq_scaled")
        misc_full, misc_done = sem("misc_full"), sem("misc_done")
        stats_done, mv_ready, var_ready, rstd_ready, xn_ready, xh_ready = (
            sem(n) for n in ("stats_done", "mv_ready", "var_ready", "rstd_ready", "xn_ready", "xh_ready"))
        rt_link, ex_ready, wd_stored = sem("rt_link"), sem("ex_ready"), sem("wd_stored")
        g_full, u_full, sg_ready, sw_ready, h_ready, h_used = (
            sem(n) for n in ("gate_full", "up_full", "silu_ready", "weighted_ready", "hidden_ready", "hidden_used"))
        y_full, y_done, x1_done, x3_done, stored = (
            sem(n) for n in ("y_full", "y_done", "x1_done", "x3_done", "stored"))
        qkv_full = [sem(f"qkv_full{i}") for i in range(2)]
        qkv_done = [sem(f"qkv_done{i}") for i in range(2)]
        v_full = [sem(f"v_full{i}") for i in range(2)]
        v_done = [sem(f"v_done{i}") for i in range(2)]
        carried, rs_full, rs_hi, rs_lo = sem("carried"), sem("rs_full"), sem("rs_hi"), sem("rs_lo")
        skew_stored = [sem(f"skew_stored{i}") for i in range(2)]
        wide_full = [sem(f"wide_full{i}") for i in range(4)]
        s_full, l_ready, p_ready, rc_ready, pn_ready, pt_full, pt_done, av_full, av_done, z_full, z_done = (
            sem(n) for n in ("scores_full", "logits_ready", "exp_ready", "recip_ready", "normed_ready",
                             "pt_full", "pt_done", "av_full", "av_done", "z_full", "z_done"))

        RT = 14

        block = ctx.enter_context(nc.Block())

        @block.sync
        def _(sp):
            def wait_all(*waits):
                for _, n in waits:
                    if not isinstance(n, int):
                        sp.compute_val(n)
                for s, n in waits:
                    sp.wait_ge(s, n)

            def load_x(g):
                sp.dma_start(x0[:, :, :], x_in[bass.ds(g * GT, GT), :].rearrange("(t p) d -> p t d", p=P)).then_inc(s_x, 16)

            def store_w(where, g, stage, f, slot):
                sp.wait_ge(misc_done, misc_use(where, g, stage, "w") + 1)
                sp.dma_start(wd[slot].rearrange("(e t) -> e t", e=E), w_t[:, :]).then_inc(wd_stored, 16)

            def spread_w(where, g, f, slot, second):
                for s in range(4):
                    waits = [(wd_stored, (f + 1) * 16)] if s == 0 else []
                    if where != "pro" and not second:
                        waits.append((l_ready, g * NH + 4 * (12 + s) + 4))
                    if second:
                        waits.append((sw_ready, (f - 1) * NCH + 4 * s + 4))
                    wait_all(*waits)
                    src = wd[slot:slot + 1, s * 1024:(s + 1) * 1024].to_broadcast([P, 1024])
                    sp.dma_start(wide[:, s, :], src).then_inc(wide_full[s], 16)

            def store_e(where, g, stage, gq, q):
                waits = [(misc_done, misc_use(where, g, stage, f"e{q}") + 1)]
                if where != "pro":
                    waits.append((wide_full[q % 4], band_uses(gq, q) * 16 - (32 if q < 4 else 0)))
                wait_all(*waits)
                d = skew[q % 4]
                dst = bass.AP(d.tensor, d.offset + 1, [[2 * P + 1, P], [2 * P * P, 4], [1, P]])
                sp.dma_start(dst, es[:, q % 2, :].rearrange("p (h j) -> p h j", h=4)).then_inc(skew_stored[q % 2], 16)

            def load_band(where, g, gq, q):
                f = 0 if where == "pro" else g * 2 + 2
                wait_all((skew_stored[q % 2], gq * (8 * NQ) + 16 * (q // 2 + 1)),
                         (l_ready, gq * NH + 4 * (q - 4) + 4) if q >= 4
                         else (sw_ready, f * NCH + 4 * q + 4))
                sp.dma_start(wide[:, q % 4, :].rearrange("p (h c) -> p h c", h=4),
                             skew[q % 4].rearrange("(h p c) -> p h c", h=4, p=P)).then_inc(wide_full[q % 4], 16)

            def store_x(g):
                sp.wait_ge(x3_done, g + 1)
                sp.dma_start(out[bass.ds(g * GT, GT), :].rearrange("(t p) d -> p t d", p=P), x2[:, :, :]).then_inc(stored, 16)

            load_x(0)
            sp.dma_start(raw_rt, wrt).then_inc(s_rt, 16)
            sp.wait_ge(zeroed, 1)
            sp.dma_start(raw_bias[BG:BU, :], bg.rearrange("e (m p) -> (e m) p", p=P)).then_inc(s_bias, 16)
            sp.dma_start(raw_bias[BU:BQ, :], bu.rearrange("e (m p) -> (e m) p", p=P)).then_inc(s_bias, 16)
            sp.dma_start(raw_bias[BQ:BP, :], bq.rearrange("(a p) -> a p", p=P)).then_inc(s_bias, 16)
            sp.dma_start(raw_bias[BP:BR, :], bproj.rearrange("(a p) -> a p", p=P)).then_inc(s_bias, 16)
            for half in range(2):
                sp.dma_start(raw_bias[BR:NBIAS, 64 * half:64 * half + 40], br.rearrange("(q c) -> q c", q=4)).then_inc(s_bias, 16)
            for e in range(E):
                sp.dma_start(raw_gu[:, e, 0, :], wg[e]).then_inc(s_gu[e], 16)
                sp.dma_start(raw_gu[:, e, 1, :], wu[e]).then_inc(s_gu[e], 16)
                if e == 1:
                    sp.dma_start(bo_s[:, :], bo).then_inc(s_bo, 16)
                    sp.dma_start(wo_s[:, :, :], wo.rearrange("e (m p) d -> p (e m) d", p=P)).then_inc(s_wo, 16)
            store_w("pro", 0, "route", 0, 0)
            spread_w("pro", 0, 0, 0, False)
            sp.wait_ge(zeroed, 3)
            for half in range(2):
                sp.dma_start(raw_r[:, :, 64 * half:64 * half + 40], wr.rearrange("d (q c) -> d q c", q=4)).then_inc(s_wr, 16)
                for h in range(4):
                    sp.dma_start(raw_b[64 * half + NB * h:64 * half + NB * h + NB, P * h:P * h + P], brev).then_inc(s_brev, 16)
            for a, wx in enumerate((wq, wk, wv)):
                sp.dma_start(raw_qkv[:, a, :], wx).then_inc(s_qkv[a], 16)
            sp.dma_start(wp_s[:, :, :], wproj.rearrange("(a p) d -> p a d", p=P)).then_inc(s_wp, 16)
            sp.wait_ge(negs_ready, 1)
            for q in range(4):
                sp.dma_start(skew[q].rearrange("(p c) -> p c", p=P), negs).then_inc(s_neg if q else stored, 16)
            sp.wait_ge(s_neg, 48)
            sp.wait_ge(stored, 16)
            for q in range(4):
                store_e("pro", 0, "qkv", 0, q)
                if q:
                    load_band("pro", 0, 0, q - 1)
            load_band("pro", 0, 0, 3)

            def attention(where, g):
                if where == "loop":
                    sp.wait_ge(x1_done, g + 1)
                    load_x(g + 1)
                for q in range(4, NQ):
                    store_e(where, g, "att", g, q)
                    if q > 4:
                        load_band(where, g, g, q - 1)
                    if q == W_STEP + 4 and where == "loop":
                        store_w(where, g, "att", g * 2 + 1, 1)
                load_band(where, g, g, NQ - 1)

            with sp.Fori(0, NGROUP - 1) as g:
                attention("loop", g)
                spread_w("loop", g, g * 2 + 1, 1, False)
                store_w("loop", g, "ffn1", g * 2 + 2, 0)
                spread_w("loop", g, g * 2 + 2, 0, True)
                for q in range(4):
                    store_e("loop", g, "qkv", g + 1, q)
                    if q:
                        load_band("loop", g, g + 1, q - 1)
                load_band("loop", g, g + 1, 3)
                store_x(g)
            last = NGROUP - 1
            attention("last", last)
            store_w("last", last, "ffn1", 2 * last + 1, 1)
            spread_w("last", last, 2 * last + 1, 1, False)
            store_x(last)
            sp.wait_ge(stored, 16 + 16 * NGROUP)
            for s in skew_stored:
                sp.wait_ge(s, 8 * NQ * NGROUP)
            sp.wait_ge(wd_stored, 16 * 2 * NGROUP)

        @block.gpsimd
        def _(pool):
            def affine(tile, pattern, base, channel, fill, op):
                return nc.gpsimd.affine_select(out=tile, in_=tile, compare_op=op, fill=fill, base=base,
                                               pattern=pattern, channel_multiplier=channel)

            nc.gpsimd.memset(raw_bias[:, :], 0.0).then_inc(zeroed, 1)
            nc.gpsimd.memset(ident[:, :], 0.0).then_inc(const_ready, 1)
            nc.gpsimd.memset(tri[:, :, :], 1.0).then_inc(const_ready, 1)
            nc.gpsimd.memset(mask, 0.0).then_inc(const_ready, 1)
            nc.gpsimd.memset(epst[:, :], EPS).then_inc(const_ready, 1)
            nc.gpsimd.memset(mhalf[:, :], -0.5).then_inc(const_ready, 1)
            pool.wait_ge(const_ready, 5)
            affine(ident[:, :], [[-1, P]], 0, 1, 1.0, ALU.not_equal).then_inc(const_ready, 1)
            affine(tri[:, :, :], [[1, E], [-1, E]], -1, 0, 0.0, ALU.is_ge).then_inc(const_ready, 1)
            affine(mask, [[1, P]], -(P - 1), 1, NEG, ALU.is_ge).then_inc(const_ready, 1)
            nc.gpsimd.memset(raw_r, 0.0).then_inc(zeroed, 1)
            nc.gpsimd.memset(raw_b, 0.0).then_inc(zeroed, 1)

            def rstd_of(n):
                pool.wait_ge(mv_ready, n + 1)
                nc.gpsimd.tensor_tensor(var[:, :], mv[:, :, 1], epst[:, :], ALU.add).then_inc(var_ready, 1)
                pool.wait_ge(var_ready, n + 1)
                nc.gpsimd.tensor_tensor(rstd[:, :], var[:, :], mhalf[:, :], ALU.pow).then_inc(rstd_ready, 1)

            def ffn(where, g, f, second, hooks):
                for c in range(NCH):
                    for hook in hooks.get(c, []):
                        hook()
                    if c == 0 and where == "loop" and not second:
                        pool.wait_ge(pn_ready, (g + 1) * NP)
                    if c % 4 == 0:
                        pool.wait_ge(wide_full[c // 4], weight_uses(where, g, second) * 16 + 16)
                    if not (where == "pro" and c < 4):
                        pool.wait_ge(h_ready, f * NCH + c - 3)
                    pool.wait_ge(sg_ready, f * NCH + c + 1)
                    wb = wide[:, c // 4, 512 * (c // 2 % 2):512 * (c // 2 % 2) + 512]
                    nc.gpsimd.tensor_tensor(sw_s[c % 4], sg_s[c % 4], wb, ALU.mult).then_inc(sw_ready, 1)

            def attention(where, g):
                for p in range(NP):
                    if p == 4 and where == "loop":
                        rstd_of(g * 3 + 2)
                    if p >= 4:
                        pool.wait_ge(pt_full, g * NP + p - 3)
                    pool.wait_ge(rc_ready, g * NP + p + 1)
                    ri = rsum[:, 2 * p:2 * p + 2].unsqueeze(2).to_broadcast([P, 2, 256])
                    nc.gpsimd.tensor_tensor(pn_s[p % 4].rearrange("p (h c) -> p h c", h=2),
                                            ex_s[p % 4].rearrange("p (h c) -> p h c", h=2),
                                            ri, ALU.mult).then_inc(pn_ready, 1)

            rstd_of(0)
            ffn("pro", 0, 0, False, {})
            nc.gpsimd.memset(negs, NEG).then_inc(negs_ready, 1)
            rstd_of(1)
            pool.wait_ge(split_lo, NPIECE)
            pool.wait_ge(s_neg, 48)
            pool.wait_ge(stored, 16)
            pool.wait_ge(misc_done, 1)
            nc.gpsimd.memset(kt[:, :, 0:P], 0.0).then_inc(kv_zeroed, 1)
            nc.gpsimd.memset(vt[:, 0, :], 0.0).then_inc(kv_zeroed, 1)
            with pool.Fori(0, NGROUP - 1) as g:
                attention("loop", g)
                ffn("loop", g, g * 2 + 1, False, {3: [lambda: rstd_of(g * 3 + 3)]})
                ffn("loop", g, g * 2 + 2, True, {3: [lambda: rstd_of(g * 3 + 4)]})
            last = NGROUP - 1
            attention("last", last)
            rstd_of(3 * last + 2)
            ffn("last", last, 2 * last + 1, False, {})

        @block.scalar
        def _(act):
            def split(i, loaded):
                for s, n in loaded:
                    act.wait_ge(s, n)
                raw, hi, _ = pieces[i]
                nc.scalar.activation(hi, raw, ACT.Copy).then_inc(split_hi, 1)

            def x_hi(where, g, stage, buf):
                act.wait_ge(misc_full, misc_use(where, g, stage, "x") + 1)
                nc.scalar.activation(xh[buf][:, :], misc[:, :], ACT.Copy).then_inc(xh_ready, 1)

            def route_exp(f):
                act.wait_ge(rt_link, f * RT + 3)
                nc.scalar.activation(ex[:, :, :], dl[:, :, :], ACT.Exp).then_inc(ex_ready, 1)

            def w_out(where, g, stage, f):
                if where != "pro":
                    act.wait_ge(wd_stored, f * 16)
                act.wait_ge(misc_full, misc_use(where, g, stage, "w") + 1)
                nc.scalar.activation(w_t[:, :], misc[0:E, :], ACT.Copy).then_inc(misc_done, 1)

            def z_out(g):
                act.wait_ge(z_full, g + 1)
                nc.scalar.activation(yz, acc[:, :], ACT.Identity, bias=bias[:, BP:BP + 1]).then_inc(z_done, 1)

            def ffn(where, f, hooks, chunks=range(NCH)):
                for c in chunks:
                    for hook in hooks.get(c, []):
                        hook()
                    if not (where == "pro" and c < 4):
                        act.wait_ge(sw_ready, f * NCH + c - 3)
                    act.wait_ge(g_full, f * NCH + c + 1)
                    nc.scalar.activation(sg_s[c % 4], bank[c % 2][:, :], ACT.Silu,
                                         bias=bias[:, BG + c:BG + c + 1]).then_inc(sg_ready, 1)
                if chunks[-1] != NCH - 1:
                    return
                act.wait_ge(y_full, f + 1)
                nc.scalar.activation(yz, acc[:, :], ACT.Copy, scale=0.5).then_inc(y_done, 1)

            def e_out(where, g, stage, gq, q):
                act.wait_ge(skew_stored[q % 2], gq * (8 * NQ) + 16 * (q // 2))
                act.wait_ge(misc_full, misc_use(where, g, stage, f"e{q}") + 1)
                nc.scalar.activation(es[:, q % 2, :], misc[:, :], ACT.Copy).then_inc(misc_done, 1)

            def qkv(where, g, gq):
                n = 0
                for i in range(NQK):
                    if i % 4 < 2:
                        act.wait_ge(qkv_full[0], gq * (NQK // 2) + n + 1)
                        src, n = bank[i % 4][:, :], n + 1
                        if i < 8:
                            nc.scalar.activation(qt[:, i, :], src, ACT.Identity, scale=0.125,
                                                 bias=bias[:, BQ + i:BQ + i + 1]).then_inc(qkv_done[0], 1)
                        else:
                            nc.scalar.activation(kt[:, i - 8, P:], src, ACT.Copy).then_inc(qkv_done[0], 1)
                    if i in (0, 2, 4, 6):
                        q = i // 2
                        act.wait_ge(rs_full, gq * 4 + q + 1)
                        nc.scalar.activation(rs[:, q, :], ptb[q % 2][:, :], ACT.Identity,
                                             bias=bias[:, BR + q:BR + q + 1]).then_inc(rs_hi, 1)
                    if i in E_AFTER and where != "pro":
                        e_out(where, g, "qkv", gq, E_AFTER.index(i))

            def v_out(g, j):
                act.wait_ge(v_full[0], g * (NV // 2) + j // 2 + 1)
                nc.scalar.activation(vt[:, 1 + j // 2, 0:512], ptb[0][:, :], ACT.Copy).then_inc(v_done[0], 1)

            def attention(where, g):
                for s in range(NQ + LAG):
                    if s == X_STEP + 1 and where == "loop":
                        x_hi(where, g, "att", 0)
                    if s == W_STEP + 1 and where == "loop":
                        w_out(where, g, "att", g * 2 + 1)
                    if s == NQ and where == "loop":
                        act.wait_ge(p_ready, (g + 1) * NH)
                        ffn(where, g * 2 + 1, {}, range(2))
                    if s < NQ:
                        if s < 2:
                            v_out(g, 4 * s)
                            v_out(g, 4 * s + 2)
                        for i in range(4):
                            n = 4 * s + i
                            if i % 2 == 0 and n >= 8:
                                act.wait_ge(pn_ready, g * NP + n // 2 - 3)
                            act.wait_ge(l_ready, g * NH + n + 1)
                            nc.scalar.activation(ex_s[n // 2 % 4][:, 256 * (i % 2):256 * (i % 2) + 256], lg_s[i],
                                                 ACT.Exp, bias=nmx[:, n:n + 1], scale=-1.0,
                                                 accum_out=sums[:, n:n + 1]).then_inc(p_ready, 1)
                    if s + 4 < NQ:
                        e_out(where, g, "att", g, s + 4)
                    if s == ROUTE_STEP + 1 and where == "loop":
                        route_exp(g * 2 + 1)
                    if s >= LAG and (s - LAG) % 2 == 1:
                        u = (s - LAG) // 2
                        act.wait_ge(av_full, g * NP + 4 * u + 4)
                        nc.scalar.activation(qt[:, 4 * (u % 2):4 * (u % 2) + 4, P * (u // 2):P * (u // 2) + P],
                                             acc[:, :].rearrange("p (a t) -> p a t", a=4),
                                             ACT.Copy).then_inc(av_done, 1)
                z_out(g)

            act.wait_ge(misc_full, 1)
            nc.scalar.activation(bias[:, 0:NBIAS], misc[:, 0:NBIAS], ACT.Copy).then_inc(misc_done, 1)
            split(0, [(s_rt, 16)])
            x_hi("pro", 0, "route", 0)
            split(1, [(s_gu[0], 32)])
            route_exp(0)
            split(2, [(s_gu[1], 32)])
            w_out("pro", 0, "route", 0)
            loads = ([[(s_gu[e], 32)] for e in range(2, E)] + [[(s_wr, 32)], [(s_brev, 128)]]
                     + [[(s_qkv[a], 16)] for a in range(3) for _ in range(2)])
            ffn("pro", 0, {c: [lambda c=c: split(3 + c, loads[c])] for c in range(len(loads))})
            x_hi("pro", 0, "ffn2", 0)
            act.wait_ge(kv_zeroed, 2)
            act.wait_ge(bq_scaled, 1)
            qkv("pro", 0, 0)
            with act.Fori(0, NGROUP - 1) as g:
                attention("loop", g)

                def carry():
                    nc.scalar.activation(kt[:, :, 0:P], kt[:, :, GT:GT + P], ACT.Copy).then_inc(carried, 1)
                    nc.scalar.activation(vt[:, 0, :], vt[:, NBLK, :], ACT.Copy).then_inc(carried, 1)

                ffn("loop", g * 2 + 1, {2: [carry], 5: [lambda: x_hi("loop", g, "ffn1", 1)],
                                        7: [lambda: route_exp(g * 2 + 2)],
                                        11: [lambda: w_out("loop", g, "ffn1", g * 2 + 2)]}, range(2, NCH))
                ffn("loop", g * 2 + 2, {5: [lambda: x_hi("loop", g, "ffn2", 0)]})
                act.wait_ge(carried, g * 2 + 2)
                qkv("loop", g, g + 1)
            last = NGROUP - 1
            attention("last", last)
            x_hi("last", last, "ffn1", 1)
            route_exp(2 * last + 1)
            w_out("last", last, "ffn1", 2 * last + 1)
            ffn("last", 2 * last + 1, {})

        @block.vector
        def _(dve):
            v = nc.vector

            def split(i):
                dve.wait_ge(split_hi, i + 1)
                raw, hi, lo = pieces[i]
                v.tensor_tensor(lo, raw, hi.bitcast(F32), ALU.subtract).then_inc(split_lo, 1)

            def stats(n, x):
                for t in range(NBLK):
                    ins = v.bn_stats(st[:, t, :], x[:, t, :])
                ins.then_inc(stats_done, 1)
                dve.wait_ge(stats_done, n + 1)
                v.memset(gate[:, 2:3], 0.0)
                for t in range(NBLK):
                    ins = v.bn_aggr(mv[:, t, :], st[:, t, :])
                ins.then_inc(mv_ready, 1)

            def normalise(n, x):
                dve.wait_ge(rstd_ready, n + 1)
                for t in range(NBLK):
                    ins = v.tensor_scalar(xn[:, t, :], x[:, t, :], mv[:, t, 0:1], rstd[:, t:t + 1],
                                          ALU.subtract, ALU.mult)
                ins.then_inc(xn_ready, 1)

            def x_lo(where, g, stage, n, buf):
                dve.wait_ge(xh_ready, n + 1)
                v.tensor_tensor(xl[buf][:, :], misc[:, :], xh[buf][:, :].bitcast(F32), ALU.subtract).then_inc(misc_done, 1)

            def residual(where, g, stage, use, new, old):
                dve.wait_ge(misc_full, misc_use(where, g, stage, use) + 1)
                v.tensor_tensor(new[:, :, :], misc[:, :].rearrange("p (t d) -> p t d", t=NBLK), old[:, :, :],
                                ALU.add).then_inc(misc_done, 1)
                dve.wait_ge(misc_done, misc_use(where, g, stage, use) + 1)

            def per_token(t):
                return t[:, :].unsqueeze(2).to_broadcast([P, NBLK, E])

            def route_a(where, g, stage, f):
                dve.wait_ge(misc_full, misc_use(where, g, stage, "route") + 1)
                v.tensor_copy(lg[:, :, :], misc[:, 0:NBLK * E].rearrange("p (t e) -> p t e", t=NBLK)).then_inc(misc_done, 1)
                dve.wait_ge(misc_done, misc_use(where, g, stage, "route") + 1)
                v.tensor_reduce(mx[:, :], lg[:, :, :], X, ALU.max).then_inc(rt_link, 1)
                dve.wait_ge(rt_link, f * RT + 1)
                v.tensor_tensor(dl[:, :, :], lg[:, :, :], per_token(mx), ALU.subtract).then_inc(rt_link, 2)

            def route_b(f, parts=(0, 1, 2)):
                n = [(3, 7, 10)[parts[0]]]

                def link(ins):
                    n[0] += 1
                    ins.then_inc(rt_link, 1)
                    dve.wait_ge(rt_link, f * RT + n[0])

                other = ex[:, :, :].unsqueeze(2).to_broadcast([P, NBLK, E, E])
                own = ex[:, :, :].unsqueeze(3).to_broadcast([P, NBLK, E, E])
                if 0 in parts:
                    dve.wait_ge(ex_ready, f + 1)
                    link(v.tensor_reduce(se[:, :], ex[:, :, :], X, ALU.add))
                    link(v.tensor_tensor(gt[:, :, :, :], other, own, ALU.is_gt))
                    link(v.tensor_tensor(eq[:, :, :, :], other, own, ALU.is_equal))
                    link(v.tensor_tensor(eq[:, :, :, :], eq[:, :, :, :],
                                         tri[:, :, :].unsqueeze(1).to_broadcast([P, NBLK, E, E]), ALU.mult))
                if 1 in parts:
                    link(v.tensor_tensor(gt[:, :, :, :], gt[:, :, :, :], eq[:, :, :, :], ALU.add))
                    link(v.tensor_reduce(rank[:, :, :], gt[:, :, :, :], X, ALU.add))
                    link(v.scalar_tensor_tensor(ew[:, :, :], rank[:, :, :], 1.5, ex[:, :, :], ALU.is_lt, ALU.mult))
                if 2 in parts:
                    link(v.tensor_reduce(s2[:, :], ew[:, :, :], X, ALU.add))
                    link(v.scalar_tensor_tensor(den[:, :], se[:, :], 1.0e-8, s2[:, :], ALU.mult, ALU.add))
                    link(v.reciprocal(rden[:, :], den[:, :]))
                    v.tensor_tensor(w[:, :, :], ew[:, :, :], per_token(rden), ALU.mult).then_inc(rt_link, 1)
                    assert n[0] + 1 == RT

            def ffn(where, f, hooks):
                for c in range(NCH):
                    for hook in hooks.get(c, []):
                        hook()
                    if c >= 4:
                        dve.wait_ge(h_used, f * (NCH - 1) + c - 3)
                    dve.wait_ge(u_full, f * NCH + c + 1)
                    dve.wait_ge(sw_ready, f * NCH + c + 1)
                    v.scalar_tensor_tensor(hd_s[c % 4], up_bank[c % 4][:, :], bias[:, BU + c:BU + c + 1],
                                           sw_s[c % 4], ALU.add, ALU.mult).then_inc(h_ready, 1)

            def qkv(where, g, gq):
                n = 0
                for i in range(NQK):
                    if i % 4 >= 2:
                        dve.wait_ge(qkv_full[1], gq * (NQK // 2) + n + 1)
                        src, n = bank[i % 4][:, :], n + 1
                        if i < 8:
                            v.tensor_scalar(qt[:, i, :], src, 0.125, bias[:, BQ + i:BQ + i + 1],
                                            ALU.mult, ALU.add).then_inc(qkv_done[1], 1)
                        else:
                            v.tensor_copy(kt[:, i - 8, P:], src).then_inc(qkv_done[1], 1)
                    if i in (0, 2, 4, 6):
                        q = i // 2
                        dve.wait_ge(rs_hi, gq * 4 + q + 1)
                        v.scalar_tensor_tensor(rs[64:P, q, :], ptb[q % 2][64:P, :], bias[64:P, BR + q:BR + q + 1],
                                               rs[64:P, q, :].bitcast(F32), ALU.add, ALU.subtract).then_inc(rs_lo, 1)
                    if i == 3 and where == "loop":
                        residual(where, g, "qkv", "y", x2, x2)
                        v.memset(gate[:, 1:2], 0.0).then_inc(x3_done, 1)
                    if i in E_AFTER and where == "pro":
                        q = E_AFTER.index(i)
                        if q >= 2:
                            dve.wait_ge(skew_stored[q % 2], 16 * (q // 2))
                        dve.wait_ge(misc_full, misc_use(where, g, "qkv", f"e{q}") + 1)
                        v.tensor_tensor(es[:, q % 2, :].rearrange("p (h j) -> p h j", h=4),
                                        misc[:, :].rearrange("p (h j) -> p h j", h=4),
                                        mask.unsqueeze(1).to_broadcast([P, 4, P]), ALU.add).then_inc(misc_done, 1)

            def v_out(g, j):
                dve.wait_ge(v_full[1], g * (NV // 2) + j // 2 + 1)
                v.tensor_copy(vt[:, 1 + j // 2, 512:1024], ptb[1][:, :]).then_inc(v_done[1], 1)

            def pt_out(g, p):
                if p >= 2:
                    dve.wait_ge(av_full, g * NP + p - 1)
                dve.wait_ge(pt_full, g * NP + p + 1)
                v.tensor_copy(pt_s[p % 2], ptb[p % 2][:, :]).then_inc(pt_done, 1)

            def recip(g, p):
                dve.wait_ge(p_ready, g * NH + 2 * p + 2)
                v.reciprocal(rsum[:, 2 * p:2 * p + 2], sums[:, 2 * p:2 * p + 2]).then_inc(rc_ready, 1)

            def attention(where, g):
                for s in range(NQ + LAG):
                    if s >= LAG:
                        pt_out(g, 2 * (s - LAG))
                    if 1 <= s <= NQ:
                        recip(g, 2 * s - 1)
                    if s >= LAG:
                        pt_out(g, 2 * (s - LAG) + 1)
                    if where == "loop":
                        if s == 1:
                            dve.wait_ge(s_x, g * 16 + 32)
                            stats(g * 3 + 2, x0)
                        if s == 3:
                            normalise(g * 3 + 2, x0)
                        if s == X_STEP + 1:
                            x_lo(where, g, "att", g * 3 + 2, 0)
                        if s == ROUTE_STEP + 1:
                            route_a(where, g, "att", g * 2 + 1)
                        if ROUTE_STEP + 2 <= s < ROUTE_STEP + 5:
                            route_b(g * 2 + 1, (s - ROUTE_STEP - 2,))
                    if s < 2:
                        v_out(g, 4 * s + 1)
                        v_out(g, 4 * s + 3)
                    if s < NQ:
                        dve.wait_ge(s_full, g * NQ + s + 1)
                        dve.wait_ge(wide_full[s % 4], band_uses(g, s) * 16 + 16)
                        if s:
                            dve.wait_ge(p_ready, g * NH + 4 * s)
                        v.memset(gate[:, 0:1], 0.0)
                        for i in range(4):
                            n = 4 * s + i
                            v.tensor_tensor_reduce(out=lg_s[i],
                                                   in0=bank[2 * (s % 2) + i % 2][:, 256 * (i // 2):256 * (i // 2) + 256],
                                                   in1=wide[:, s % 4, 256 * i:256 * i + 256],
                                                   scale=-1.0, scalar=3.0e38, op0=ALU.add, op1=ALU.min,
                                                   accum_out=nmx[:, n:n + 1]).then_inc(l_ready, 1)
                        recip(g, 2 * s)

            dve.wait_ge(s_x, 16)
            stats(0, x0)
            normalise(0, x0)
            split(0)
            dve.wait_ge(misc_done, 1)
            v.tensor_scalar(bias[:, BQ:BP], bias[:, BQ:BP], 0.125, None, ALU.mult).then_inc(bq_scaled, 1)
            x_lo("pro", 0, "route", 0, 0)
            split(1)
            route_a("pro", 0, "route", 0)
            route_b(0)
            split(2)
            ffn("pro", 0, {c: [lambda c=c: split(3 + c)] for c in range(NPIECE - 3)})
            residual("pro", 0, "ffn2", "y", x1, x0)
            v.memset(gate[:, 1:2], 0.0).then_inc(x1_done, 1)
            stats(1, x1)
            normalise(1, x1)
            x_lo("pro", 0, "ffn2", 1, 0)
            dve.wait_ge(kv_zeroed, 2)
            dve.wait_ge(bq_scaled, 1)
            qkv("pro", 0, 0)
            with dve.Fori(0, NGROUP - 1) as g:
                attention("loop", g)

                def tail2():
                    dve.wait_ge(stored, g * 16 + 16)
                    residual("loop", g, "ffn1", "z", x2, x1)
                    stats(g * 3 + 3, x2)

                def tail1():
                    residual("loop", g, "ffn2", "y", x1, x0)
                    v.memset(gate[:, 1:2], 0.0).then_inc(x1_done, 1)
                    stats(g * 3 + 4, x1)

                ffn("loop", g * 2 + 1, {2: [tail2], 4: [lambda: normalise(g * 3 + 3, x2)],
                                        5: [lambda: x_lo("loop", g, "ffn1", g * 3 + 3, 1)],
                                        7: [lambda: route_a("loop", g, "ffn1", g * 2 + 2)],
                                        8: [lambda: route_b(g * 2 + 2, (0,))],
                                        9: [lambda: route_b(g * 2 + 2, (1,))],
                                        10: [lambda: route_b(g * 2 + 2, (2,))]})
                ffn("loop", g * 2 + 2, {2: [tail1], 4: [lambda: normalise(g * 3 + 4, x1)],
                                        5: [lambda: x_lo("loop", g, "ffn2", g * 3 + 4, 0)]})
                dve.wait_ge(carried, g * 2 + 2)
                qkv("loop", g, g + 1)
            last = NGROUP - 1
            attention("last", last)
            dve.wait_ge(stored, last * 16 + 16)
            residual("last", last, "ffn1", "z", x2, x1)
            stats(3 * last + 2, x2)
            normalise(3 * last + 2, x2)
            x_lo("last", last, "ffn1", 3 * last + 2, 1)
            route_a("last", last, "ffn1", 2 * last + 1)
            route_b(2 * last + 1)
            ffn("last", 2 * last + 1, {})
            residual("last", last, "end", "y", x2, x2)
            v.memset(gate[:, 1:2], 0.0).then_inc(x3_done, 1)

        @block.tensor
        def _(pe):
            mm = nc.tensor.matmul

            def three(out_ap, w_hi, w_lo, m_hi, m_lo):
                mm(out_ap, w_hi, m_hi, start=True, stop=False)
                mm(out_ap, w_lo, m_hi, start=False, stop=False)
                return mm(out_ap, w_hi, m_lo, start=False, stop=True)

            def claim(where, g, stage, use):
                n = misc_use(where, g, stage, use)
                if not (where == "pro" and n == 0):
                    pe.wait_ge(misc_done, n)

            def turn(src):
                for t in range(NBLK):
                    ins = nc.tensor.transpose(misc[:, P * t:P * t + P], src(t), ident[:, :])
                ins.then_inc(misc_full, 1)

            def x_turn(where, g, stage, n):
                claim(where, g, stage, "x")
                pe.wait_ge(xn_ready, n + 1)
                turn(lambda t: xn[:, t, :])

            def back(where, g, stage, use, s, count):
                claim(where, g, stage, use)
                pe.wait_ge(s, count)
                turn(lambda t: yz[:, P * t:P * t + P])

            def route(where, g, stage, buf):
                claim(where, g, stage, "route")
                for t in range(NBLK):
                    xt = slice(P * t, P * t + P)
                    o = misc[:, E * t:E * t + E]
                    mm(o, xh[buf][:, xt], rt_hi[:, :], start=True, stop=False)
                    mm(o, xl[buf][:, xt], rt_hi[:, :], start=False, stop=False)
                    ins = mm(o, xh[buf][:, xt], rt_lo[:, :], start=False, stop=True)
                ins.then_inc(misc_full, 1)

            def w_turn(where, g, stage, f):
                claim(where, g, stage, "w")
                pe.wait_ge(rt_link, f * RT + RT)
                for t in range(NBLK):
                    ins = nc.tensor.transpose(misc[0:E, P * t:P * t + P], w[:, t, :], ident[:, :])
                ins.then_inc(misc_full, 1)

            def ffn(where, f, buf, x_use, w_use, acc_free, hooks, chunks=range(NCH + 3), scores_read=None):
                for c in chunks:
                    for hook in hooks.get(c, []):
                        hook()
                    if c < NCH:
                        e, m = c // 2, P * (c % 2)
                        if c == 0:
                            pe.wait_ge(misc_done, x_use + 1)
                        if where == "pro" and c % 2 == 0:
                            pe.wait_ge(split_lo, 2 + e)
                        if not (where == "pro" and c < 2):
                            pe.wait_ge(sg_ready, f * NCH + c - 1)
                        three(bank[c % 2][:, :], gu_hi[:, e, 0, m:m + P], gu_lo[:, e, 0, m:m + P],
                              xh[buf][:, :], xl[buf][:, :]).then_inc(g_full, 1)
                        if scores_read is not None:
                            pe.wait_ge(l_ready, scores_read)
                        elif not (where == "pro" and c < 4):
                            pe.wait_ge(h_ready, f * NCH + c - 3)
                        three(up_bank[c % 4][:, :], gu_hi[:, e, 1, m:m + P], gu_lo[:, e, 1, m:m + P],
                              xh[buf][:, :], xl[buf][:, :]).then_inc(u_full, 1)
                    if c == 2:
                        pe.wait_ge(misc_done, w_use + 1)
                        if acc_free:
                            pe.wait_ge(*acc_free)
                        if where == "pro":
                            pe.wait_ge(s_bo, 16)
                            pe.wait_ge(s_wo, 16)
                        mm(acc[:, :], bo_s[:, :], w_t[:, :], start=True, stop=False)
                    if c >= 3:
                        pe.wait_ge(h_ready, f * NCH + c - 2)
                        ins = mm(acc[:, :], wo_s[:, c - 3, :], hd_s[(c - 3) % 4], start=False, stop=(c == NCH + 2))
                        ins.then_inc(y_full if c == NCH + 2 else h_used, 1)

            def e_mm(where, g, stage, q):
                claim(where, g, stage, f"e{q}")
                blk = slice(P * (q // 4), P * (q // 4) + P)
                mm(misc[:, :], rs[:, q % 4, blk], b_hi[:, :], start=True, stop=False)
                mm(misc[:, :], rs[:, q % 4, blk], b_lo[:, :], start=False, stop=True).then_inc(misc_full, 1)

            def qkv(where, g, gq, f):
                n = [0, 0]
                if where == "pro":
                    pe.wait_ge(split_lo, NPIECE)
                for i in range(NQK):
                    side = i % 4 // 2
                    if i >= 4:
                        pe.wait_ge(qkv_done[side], gq * (NQK // 2) + n[side] - 1)
                    a, c = i // 8, P * (i % 8)
                    three(bank[i % 4][:, :], qkv_hi[:, a, c:c + P], qkv_lo[:, a, c:c + P],
                          xh[0][:, :], xl[0][:, :]).then_inc(qkv_full[side], 1)
                    n[side] += 1
                    if i in (0, 2, 4, 6):
                        q = i // 2
                        if q >= 2:
                            pe.wait_ge(rs_lo, gq * 4 + q - 1)
                        three(ptb[q % 2][:, :], r_hi[:, q, :], r_lo[:, q, :], xh[0][:, :], xl[0][:, :]).then_inc(rs_full, 1)
                    if i == 3 and where == "loop":
                        back(where, g, "qkv", "y", y_done, f + 1)
                    if i in E_AFTER:
                        if i == E_AFTER[0]:
                            pe.wait_ge(rs_lo, gq * 4 + 4)
                        e_mm(where, g, "qkv", E_AFTER.index(i))

            def values(g, j):
                if j >= 2:
                    pe.wait_ge(v_done[j % 2], g * (NV // 2) + j // 2)
                else:
                    pe.wait_ge(rs_lo, g * 4 + 4)
                t, c = P * (j // 2), 512 * (j % 2)
                three(ptb[j % 2][:, :], xh[0][:, t:t + P], xl[0][:, t:t + P],
                      qkv_hi[:, 2, c:c + 512], qkv_lo[:, 2, c:c + 512]).then_inc(v_full[j % 2], 1)

            def scores(g, s):
                b = s // 4
                if s >= 2:
                    pe.wait_ge(l_ready, g * NH + 4 * (s - 1))
                for jj in range(2):
                    j = 2 * (s % 4) + jj
                    for hh in range(2):
                        r = slice(64 * hh, 64 * hh + 64)
                        ins = mm(bank[2 * (s % 2) + hh][:, 256 * jj:256 * jj + 256], qt[r, j, P * b:P * b + P],
                                 kt[r, j, P * b:P * b + 2 * P], start=True, stop=True)
                ins.then_inc(s_full, 1)

            def pt(g, p):
                pe.wait_ge(pn_ready, g * NP + p + 1)
                if p >= 2:
                    pe.wait_ge(pt_done, g * NP + p - 1)
                for k in range(4):
                    ins = nc.tensor.transpose(ptb[p % 2][:, P * k:P * k + P], pn_s[p % 4][:, P * k:P * k + P], ident[:, :])
                ins.then_inc(pt_full, 1)

            def av(g, p):
                b, j = p // 8, p % 8
                if p % 4 == 0 and p:
                    pe.wait_ge(av_done, g * (NP // 4) + p // 4)
                if p == 0:
                    pe.wait_ge(y_done, g * 2 + 1)
                pe.wait_ge(pt_done, g * NP + p + 1)
                for k in range(2):
                    for hh in range(2):
                        ins = mm(acc[64 * hh:64 * hh + 64, P * (p % 4):P * (p % 4) + P],
                                 vt[:, b + k, P * j + 64 * hh:P * j + 64 * hh + 64],
                                 pt_s[p % 2][:, 256 * hh + P * k:256 * hh + P * k + P], start=(k == 0), stop=(k == 1))
                ins.then_inc(av_full, 1)

            def attention(where, g):
                for side in range(2):
                    pe.wait_ge(qkv_done[side], (g + 1) * (NQK // 2))
                for s in range(NQ + LAG):
                    p0 = 2 * (s - LAG)
                    if s == LAG:
                        for side in range(2):
                            pe.wait_ge(v_done[side], (g + 1) * (NV // 2))
                    if s >= LAG:
                        pt(g, p0)
                        pt(g, p0 + 1)
                    if s < NQ:
                        scores(g, s)
                    if s >= LAG:
                        av(g, p0)
                    if s + 4 < NQ:
                        e_mm(where, g, "att", s + 4)
                    if s >= LAG:
                        av(g, p0 + 1)
                    if s < 2:
                        for j in range(4 * s, 4 * s + 4):
                            values(g, j)
                    if where == "loop":
                        if s == X_STEP:
                            x_turn(where, g, "att", g * 3 + 2)
                        if s == ROUTE_STEP:
                            route(where, g, "att", 0)
                        if s == W_STEP:
                            w_turn(where, g, "att", g * 2 + 1)
                        if s >= NQ - 1 and s < NQ + 1:
                            ffn(where, g * 2 + 1, 0, misc_use(where, g, "att", "x"), misc_use(where, g, "att", "w"),
                                None, {}, range(s - NQ + 1, s - NQ + 2), (g + 1) * NH)
                pe.wait_ge(av_done, (g + 1) * (NP // 4))
                for j in range(NPAIR):
                    ins = mm(acc[:, :], wp_s[:, j, :], qt[:, j, :], start=(j == 0), stop=(j == NPAIR - 1))
                ins.then_inc(z_full, 1)

            pe.wait_ge(const_ready, 8)
            pe.wait_ge(s_bias, 96)
            nc.tensor.transpose(misc[:, 0:NBIAS], raw_bias[0:NBIAS, :], ident[0:NBIAS, 0:NBIAS]).then_inc(misc_full, 1)
            x_turn("pro", 0, "route", 0)
            pe.wait_ge(split_lo, 1)
            route("pro", 0, "route", 0)
            w_turn("pro", 0, "route", 0)
            ffn("pro", 0, 0, misc_use("pro", 0, "route", "x"), misc_use("pro", 0, "route", "w"), None, {})
            back("pro", 0, "ffn2", "y", y_done, 1)
            x_turn("pro", 0, "ffn2", 1)
            pe.wait_ge(misc_done, misc_use("pro", 0, "ffn2", "x") + 1)
            pe.wait_ge(s_wp, 16)
            qkv("pro", 0, 0, 0)
            with pe.Fori(0, NGROUP - 1) as g:
                attention("loop", g)
                ffn("loop", g * 2 + 1, 0, misc_use("loop", g, "att", "x"), misc_use("loop", g, "att", "w"),
                    (z_done, g + 1),
                    {3: [lambda: back("loop", g, "ffn1", "z", z_done, g + 1)],
                     5: [lambda: x_turn("loop", g, "ffn1", g * 3 + 3)],
                     7: [lambda: route("loop", g, "ffn1", 1)],
                     11: [lambda: w_turn("loop", g, "ffn1", g * 2 + 2)]}, range(2, NCH + 3))
                ffn("loop", g * 2 + 2, 1, misc_use("loop", g, "ffn1", "x"), misc_use("loop", g, "ffn1", "w"),
                    (y_done, g * 2 + 2),
                    {2: [lambda: back("loop", g, "ffn2", "y", y_done, g * 2 + 2)],
                     5: [lambda: x_turn("loop", g, "ffn2", g * 3 + 4)]})
                pe.wait_ge(misc_done, misc_use("loop", g, "ffn2", "x") + 1)
                qkv("loop", g, g + 1, g * 2 + 2)
            last = NGROUP - 1
            attention("last", last)
            back("last", last, "ffn1", "z", z_done, last + 1)
            x_turn("last", last, "ffn1", 3 * last + 2)
            route("last", last, "ffn1", 1)
            w_turn("last", last, "ffn1", 2 * last + 1)
            ffn("last", 2 * last + 1, 1, misc_use("last", last, "ffn1", "x"), misc_use("last", last, "ffn1", "w"),
                (z_done, last + 1), {})
            back("last", last, "end", "y", y_done, 2 * last + 2)


_INS = ["L0_attn_X", "L0_attn_Wq", "L0_attn_bq", "L0_attn_Wk", "L0_attn_Wv", "L0_attn_Wproj", "L0_attn_bproj",
        "L0_attn_Wr", "L0_attn_br", "L0_attn_b_nd", "L0_ffn_W_router", "L0_ffn_W_gate", "L0_ffn_b_gate",
        "L0_ffn_W_up", "L0_ffn_b_up", "L0_ffn_W_out", "L0_ffn_b_out"]


def kernel(**inputs):
    import numpy as _np
    import concourse.bacc as _bacc
    from concourse import mybir as _mybir
    from concourse.bass_utils import run_bass_kernel_spmd as _run

    nc = _bacc.Bacc("TRN2", target_bir_lowering=False, num_devices=1)
    arrays, args = {}, []
    for name in _INS:
        a = _np.asarray(inputs[name])
        if name == "L0_attn_X":
            a = a.reshape(T, D)
        if name == "L0_attn_b_nd":
            a = a[:, ::-1]
        a = _np.ascontiguousarray(a)
        arrays[f"in_{name}"] = a
        args.append(nc.dram_tensor(f"in_{name}", a.shape, _mybir.dt.from_np(a.dtype), kind="ExternalInput").ap())
    args.append(nc.dram_tensor("out_0", (T, D), _mybir.dt.float32, kind="ExternalOutput").ap())
    macaron(nc, *args)
    r = _run(nc, [arrays], core_ids=[0])
    return r.results[0]["out_0"].reshape(1, T, D)
```

```python
from contextlib import ExitStack

import concourse.bass as bass
from concourse import mybir

ALU = mybir.AluOpType
ACT = mybir.ActivationFunctionType
F32 = mybir.dt.float32
F32R = mybir.dt.float32r
X = mybir.AxisListType.X

P = 128
T, D = 2048, 128
GT = 512
NGROUP = T // GT
NBLK = GT // P
E, M = 8, 256
NCH = E * M // P
H, DQ, NB = 16, 64, 10
NR = 4 * NB
STACK = ((0, 0, NR), (NR, 0, 64 - NR), (64, 0, NR), (64 + NR, 64 - NR, NR))
NPAIR = H // 2
NQ = 4 * NBLK
NP = 2 * NQ
NH = 4 * NQ
NQK = 16
NV = 8
E_AFTER = (9, 11, 13, 15)
V_SIDE = (0, 1, 1, 0, 0, 1, 1, 0)
DLAG = 5
LAG = 2
NEG = -1.0e9
EPS = 1.0e-5

USES_SETUP = ["bias"]
USES_ROUTE = ["x", "route", "w", "b0", "b1"]
USES_TAIL1 = ["y", "x"]
USES_TAIL2 = ["z", "x", "route", "w"]
USES_LAST2 = ["z", "x", "route", "w", "b0", "b1"]
USES_ATT_LAST = [f"e{q}" for q in range(4, NQ)]
X_STEP, ROUTE_STEP, W_STEP = 4, 6, 12
E_LATE = (X_STEP + 1, ROUTE_STEP + 1)
USES_ATT = [u for s in range(NQ) for u in
            [f"e{s + 4}" for _ in range(s < NQ - 4)] + [n for n, at in (("x", X_STEP), ("route", ROUTE_STEP), ("w", W_STEP)) if at == s]]
USES_QKV0 = ["e0", "e1", "e2", "e3"]
USES_QKV = ["y"] + USES_QKV0
ORDER_PROLOGUE = [("setup", USES_SETUP), ("route", USES_ROUTE), ("ffn2", USES_TAIL1), ("qkv", USES_QKV0)]
ORDER_LOOP = [("att", USES_ATT), ("ffn1", USES_TAIL2), ("ffn2", USES_TAIL1), ("qkv", USES_QKV)]
ORDER_LAST = [("att", USES_ATT_LAST), ("ffn1", USES_LAST2), ("end", ["y"])]
N_PROLOGUE = sum(len(u) for _, u in ORDER_PROLOGUE)
N_LOOP = sum(len(u) for _, u in ORDER_LOOP)


def misc_use(where, g, stage, use):
    order, base = {"pro": (ORDER_PROLOGUE, 0), "loop": (ORDER_LOOP, g * N_LOOP + N_PROLOGUE),
                   "last": (ORDER_LAST, (NGROUP - 1) * N_LOOP + N_PROLOGUE)}[where]
    for name, uses in order:
        if name == stage:
            return base + uses.index(use)
        base = base + len(uses)
    raise KeyError(stage)


def stacked_heads(c0, c1):
    found = [(h, max(c0 - NB * h, 0), min(c1 - NB * h, NB)) for h in range(4)]
    return [(h, n0, n1) for h, n0, n1 in found if n0 < n1]


def v_count(j):
    return V_SIDE[:j + 1].count(V_SIDE[j])


def band_uses(g, q):
    return g * 6 + (1 if q < 4 else 1 + q // 4)


def weight_uses(where, g, second):
    return 0 if where == "pro" else g * 6 + 5 + (1 if second and where == "loop" else 0)


def macaron(nc, x_in, wq, bq, wk, wv, wproj, bproj, wr, br, brev, wrt, wg, bg, wu, bu, wo, bo, out):
    with ExitStack() as ctx:
        def sb(name, shape, dt=F32):
            return ctx.enter_context(nc.sbuf_tensor(name, shape, dt))

        def sem(name):
            return ctx.enter_context(nc.semaphore(name))

        skew = nc.dram_tensor("skew", (4, 4 * P * 2 * P), F32, kind="Internal").ap()
        wd = nc.dram_tensor("wd", (2, E * GT), F32, kind="Internal").ap()

        bank = [ctx.enter_context(nc.psum_tensor(f"bank{i}", [P, 512], F32)) for i in range(8)]
        acc, misc, ptb = bank[4], bank[5], bank[6:8]
        up_bank, v_bank = [bank[2], bank[3], bank[6], bank[7]], [bank[6], bank[7], acc]

        gu_hi, gu_lo = sb("gu_hi", [P, E, 2, M], F32R), sb("gu_lo", [P, E, 2, M], F32R)
        qkv_hi, qkv_lo = sb("qkv_hi", [P, 3, H * DQ], F32R), sb("qkv_lo", [P, 3, H * DQ], F32R)
        r_hi, r_lo = sb("r_hi", [P, 4, P], F32R), sb("r_lo", [P, 4, P], F32R)
        rt_hi, rt_lo = sb("rt_hi", [P, E], F32R), sb("rt_lo", [P, E], F32R)
        b_mix = sb("b_mix", [P, 4 * P], F32R)
        wo_hi, wo_lo = sb("wo_hi", [P, NCH, D], F32R), sb("wo_lo", [P, NCH, D], F32R)
        wp_s, bo_s = sb("wp_s", [P, NPAIR, D]), sb("bo_s", [E, D])
        bias = sb("bias", [P, 48])
        x0, x1, x2 = (sb(f"x{i}", [P, NBLK, D]) for i in range(3))
        xn = sb("xn", [P, NBLK, D])
        xh = [sb("xh_a", [P, GT], F32R), sb("xh_b", [P, GT], F32R)]
        xl = [sb("xl_a", [P, GT], F32R), sb("xl_b", [P, GT], F32R)]
        yz = xn[:, :, :].rearrange("p t d -> p (t d)")
        qt, kt, vt = sb("qt", [P, NPAIR, GT]), sb("kt", [P, NPAIR, GT + P]), sb("vt", [P, NBLK + 1, H * DQ])
        rs = sb("rs", [P, 4, GT], F32R)
        hid_lo = sb("hid_lo", [P, 3, GT], F32R)
        es = sb("es", [P, 2, 4 * P])
        wide = sb("wide", [P, 4, 4 * 2 * P])
        work = sb("work", [P, 6144])
        lg_s = [work[:, 256 * i:256 * i + 256] for i in range(4)]
        ex_s = [work[:, 1024 + 512 * i:1536 + 512 * i] for i in range(4)]
        pn_s = [work[:, 3072 + 512 * i:3584 + 512 * i] for i in range(4)]
        pt_s = [work[:, 5120 + 512 * i:5632 + 512 * i] for i in range(2)]
        sg_s = [work[:, 512 * i:512 * i + 512] for i in range(4)]
        sw_s = [work[:, 2048 + 512 * i:2560 + 512 * i] for i in range(4)]
        hd_s = [work[:, 4096 + 512 * i:4608 + 512 * i] for i in range(4)]
        ident, tri = sb("ident", [P, P]), sb("tri", [P, E, E])
        mask = x2[:, 0, :]
        epst, mhalf, gate = sb("epst", [P, NBLK]), sb("mhalf", [P, NBLK]), sb("gate", [P, 5])
        warm = sb("warm", [P, 1])
        st, mv, var, rstd = sb("st", [P, NBLK, 6]), sb("mv", [P, NBLK, 2]), sb("var", [P, NBLK]), sb("rstd", [P, NBLK])
        nmx, sums, rsum = sb("nmx", [P, NH]), sb("sums", [P, NH]), sb("rsum", [P, NH])
        lg, mx, dl, ex = sb("lg", [P, NBLK, E]), sb("mx", [P, NBLK]), sb("dl", [P, NBLK, E]), sb("ex", [P, NBLK, E])
        se, s2, den, rden = (sb(n, [P, NBLK]) for n in ("se", "s2", "den", "rden"))
        gt, eq = sb("gt", [P, NBLK, E, E]), sb("eq", [P, NBLK, E, E])
        rank, ew, w = sb("rank", [P, NBLK, E]), sb("ew", [P, NBLK, E]), sb("w", [P, NBLK, E])
        w_t = sb("w_t", [E, GT])

        raw_gu = qt[:, :, :].rearrange("p a b -> p (a b)").rearrange("p (e a m) -> p e a m", e=E, a=2)
        raw_v = vt[:, :, :].rearrange("p a b -> p (a b)")
        raw_qkv = raw_v[:, 1024:4096].rearrange("p (a n) -> p a n", a=3)
        raw_r = raw_v[:, 4096:4608].rearrange("p (q c) -> p q c", q=4)
        raw_rt = raw_v[:, 4608:4616]
        raw_b = kt[:, 0:1, :].rearrange("p a b -> p (a b)")[:, 0:512]
        raw_bias = kt[:, 1:2, :].rearrange("p a b -> p (a b)")[:, 0:128]
        raw_wo = kt[:, 4:8, :].rearrange("p a b -> p (a b)")[:, 0:2048]
        negs = kt[:, 2:4, :].rearrange("p a b -> p (a b)")[:, 0:1024]
        BG, BU, BQ, BP, BR, NBIAS = 0, 16, 32, 40, 41, 45

        def flat(t):
            return t.rearrange("p a b -> p (a b)")

        order = ["rt", "gu0", "gu1", "wo0", "gu2", "gu3", "wo1", "gu4", "gu5", "wo2", "gu6", "qkv0", "gu7",
                 "qkv1", "wo3", "qkv2", "r", "qkv3", "b", "qkv4", "qkv5"]
        piece = {"rt": (raw_rt, rt_hi[:, :], rt_lo[:, :]), "r": (flat(raw_r), flat(r_hi[:, :, :]), flat(r_lo[:, :, :])),
                 "b": (raw_b, b_mix[:, :], b_mix[:, :])}
        for i in range(E):
            piece[f"gu{i}"] = (flat(raw_gu[:, i]), flat(gu_hi[:, i]), flat(gu_lo[:, i]))
        for i in range(4):
            piece[f"wo{i}"] = (raw_wo[:, 512 * i:512 * i + 512], flat(wo_hi[:, 4 * i:4 * i + 4, :]),
                               flat(wo_lo[:, 4 * i:4 * i + 4, :]))
        for i in range(6):
            a, n = i // 2, 512 * (i % 2)
            piece[f"qkv{i}"] = (raw_qkv[:, a, n:n + 512], qkv_hi[:, a, n:n + 512], qkv_lo[:, a, n:n + 512])
        pieces = [piece[name] for name in order]
        NPIECE = len(pieces)

        def on_pool(name):
            return name.startswith("qkv")

        def split_count(name):
            return sum(on_pool(n) == on_pool(name) for n in order[:order.index(name) + 1])

        first = [3 + c + (c > 0) + (c > 9) for c in range(NCH + 1)]
        split_at = [range(first[c], min(first[c + 1], NPIECE)) for c in range(NCH)]
        assert first[NCH] >= NPIECE

        s_x, s_rt, s_bias, s_wo, s_wp, s_bo, s_wr, s_brev, s_neg = (
            sem(n) for n in ("x_loaded", "router_loaded", "bias_loaded", "wo_loaded", "wproj_loaded",
                             "bo_loaded", "wr_loaded", "brev_loaded", "skew_filled"))
        s_gu = [sem(f"gu_loaded{e}") for e in range(E)]
        s_qkv = [sem(f"qkv_loaded{a}") for a in range(3)]
        zeroed, const_ready, negs_ready = sem("zeroed"), sem("const_ready"), sem("negs_ready")
        split_hi, split_lo, kv_zeroed = sem("split_hi"), sem("split_lo"), sem("kv_zeroed")
        split_lo_pool = sem("split_lo_pool")
        bq_scaled = sem("bq_scaled")
        misc_full, misc_done = sem("misc_full"), sem("misc_done")
        stats_done, mv_ready, var_ready, rstd_ready, xn_ready, xh_ready = (
            sem(n) for n in ("stats_done", "mv_ready", "var_ready", "rstd_ready", "xn_ready", "xh_ready"))
        rt_link, ex_ready, wd_stored = sem("rt_link"), sem("ex_ready"), sem("wd_stored")
        hh_ready, hl_ready = sem("hidden_hi_ready"), sem("hidden_lo_ready")
        g_full, u_full, sg_ready, sw_ready, h_ready, h_used = (
            sem(n) for n in ("gate_full", "up_full", "silu_ready", "weighted_ready", "hidden_ready", "hidden_used"))
        y_full, y_done, x1_done, x3_done, stored = (
            sem(n) for n in ("y_full", "y_done", "x1_done", "x3_done", "stored"))
        qkv_full = [sem(f"qkv_full{i}") for i in range(2)]
        qkv_done = [sem(f"qkv_done{i}") for i in range(2)]
        v_full = [sem(f"v_full{i}") for i in range(2)]
        v_done = [sem(f"v_done{i}") for i in range(2)]
        carried, rs_full, rs_hi, rs_lo = sem("carried"), sem("rs_full"), sem("rs_hi"), sem("rs_lo")
        skew_stored = [sem(f"skew_stored{i}") for i in range(2)]
        wide_full = [sem(f"wide_full{i}") for i in range(4)]
        s_full, l_ready, p_ready, rc_ready, pn_ready, pt_full, pt_done, av_full, av_done, z_full, z_done = (
            sem(n) for n in ("scores_full", "logits_ready", "exp_ready", "recip_ready", "normed_ready",
                             "pt_full", "pt_done", "av_full", "av_done", "z_full", "z_done"))

        RT = 14

        block = ctx.enter_context(nc.Block())

        @block.sync
        def _(sp):
            def wait_all(*waits):
                for _, n in waits:
                    if not isinstance(n, int):
                        sp.compute_val(n)
                for s, n in waits:
                    sp.wait_ge(s, n)

            def load_x(g):
                sp.dma_start(x0[:, :, :], x_in[bass.ds(g * GT, GT), :].rearrange("(t p) d -> p t d", p=P)).then_inc(s_x, 16)

            def store_w(where, g, stage, f, slot):
                sp.wait_ge(misc_done, misc_use(where, g, stage, "w") + 1)
                sp.dma_start(wd[slot].rearrange("(e t) -> e t", e=E), w_t[:, :]).then_inc(wd_stored, 16)

            def spread_w(where, g, f, slot, second):
                first = 0 if where == "loop" else 1
                for s in range(first, 4):
                    waits = [(wd_stored, (f + 1) * 16)] if s == first else []
                    if where != "pro" and not second:
                        waits.append((l_ready, g * NH + 4 * (12 + s) + 4))
                    if second:
                        waits.append((sw_ready, (f - 1) * NCH + 4 * s + 4))
                    wait_all(*waits)
                    src = wd[slot:slot + 1, s * 1024:(s + 1) * 1024].to_broadcast([P, 1024])
                    sp.dma_start(wide[:, s, :], src).then_inc(wide_full[s], 16)

            def store_e(where, g, stage, gq, q):
                waits = [(misc_done, misc_use(where, g, stage, f"e{q}") + 1)]
                if where != "pro":
                    waits.append((wide_full[q % 4], band_uses(gq, q) * 16 - (32 if q < 4 else 0)))
                wait_all(*waits)
                d = skew[q % 4]
                dst = bass.AP(d.tensor, d.offset + 1, [[2 * P + 1, P], [2 * P * P, 4], [1, P]])
                sp.dma_start(dst, es[:, q % 2, :].rearrange("p (h j) -> p h j", h=4)).then_inc(skew_stored[q % 2], 16)

            def load_band(where, g, gq, q):
                f = 0 if where == "pro" else g * 2 + 2
                wait_all((skew_stored[q % 2], gq * (8 * NQ) + 16 * (q // 2 + 1)),
                         (l_ready, gq * NH + 4 * (q - 4) + 4) if q >= 4
                         else (sw_ready, f * NCH + 4 * q + 4))
                sp.dma_start(wide[:, q % 4, :].rearrange("p (h c) -> p h c", h=4),
                             skew[q % 4].rearrange("(h p c) -> p h c", h=4, p=P)).then_inc(wide_full[q % 4], 16)

            def store_x(g):
                sp.wait_ge(x3_done, g + 1)
                sp.dma_start(out[bass.ds(g * GT, GT), :].rearrange("(t p) d -> p t d", p=P), x2[:, :, :]).then_inc(stored, 16)

            load_x(0)
            sp.dma_start(raw_rt, wrt).then_inc(s_rt, 16)
            sp.wait_ge(zeroed, 1)
            sp.dma_start(raw_bias[BG:BU, :], bg.rearrange("e (m p) -> (e m) p", p=P)).then_inc(s_bias, 16)
            sp.dma_start(raw_bias[BU:BQ, :], bu.rearrange("e (m p) -> (e m) p", p=P)).then_inc(s_bias, 16)
            sp.dma_start(raw_bias[BQ:BP, :], bq.rearrange("(a p) -> a p", p=P)).then_inc(s_bias, 16)
            sp.dma_start(raw_bias[BP:BR, :], bproj.rearrange("(a p) -> a p", p=P)).then_inc(s_bias, 16)
            for row, c0, c1 in STACK:
                sp.dma_start(raw_bias[BR:NBIAS, row:row + c1 - c0],
                             br.rearrange("(q c) -> q c", q=4)[:, c0:c1]).then_inc(s_bias, 16)
            for e in range(E):
                sp.dma_start(raw_gu[:, e, 0, :], wg[e]).then_inc(s_gu[e], 16)
                sp.dma_start(raw_gu[:, e, 1, :], wu[e]).then_inc(s_gu[e], 16)
                if e == 1:
                    sp.dma_start(bo_s[:, :], bo).then_inc(s_bo, 16)
                    sp.dma_start(raw_wo.rearrange("p (c d) -> p c d", d=D), wo.rearrange("e (m p) d -> p (e m) d", p=P)).then_inc(s_wo, 16)
            store_w("pro", 0, "route", 0, 0)
            spread_w("pro", 0, 0, 0, False)
            sp.wait_ge(zeroed, 3)
            for a, wx in enumerate((wq, wk, wv)):
                sp.dma_start(raw_qkv[:, a, :], wx).then_inc(s_qkv[a], 16)
            for row, c0, c1 in STACK:
                sp.dma_start(raw_r[:, :, row:row + c1 - c0],
                             wr.rearrange("d (q c) -> d q c", q=4)[:, :, c0:c1]).then_inc(s_wr, 16)
                for h, n0, n1 in stacked_heads(c0, c1):
                    at = row + NB * h + n0 - c0
                    sp.dma_start(raw_b[at:at + n1 - n0, P * h:P * h + P], brev[n0:n1, :]).then_inc(s_brev, 16)
            sp.dma_start(wp_s[:, :, :], wproj.rearrange("(a p) d -> p a d", p=P)).then_inc(s_wp, 16)
            sp.wait_ge(negs_ready, 1)
            for q in range(4):
                sp.dma_start(skew[q].rearrange("(p c) -> p c", p=P), negs).then_inc(s_neg if q else stored, 16)
            sp.wait_ge(s_neg, 48)
            sp.wait_ge(stored, 16)
            for q in range(4):
                store_e("pro", 0, "qkv", 0, q)
                if q:
                    load_band("pro", 0, 0, q - 1)
            load_band("pro", 0, 0, 3)

            def attention(where, g):
                if where == "loop":
                    sp.wait_ge(x1_done, g + 1)
                    load_x(g + 1)
                for q in range(4, NQ):
                    store_e(where, g, "att", g, q)
                    if q > 4:
                        load_band(where, g, g, q - 1)
                load_band(where, g, g, NQ - 1)
                if where == "loop":
                    store_w(where, g, "att", g * 2 + 1, 1)

            with sp.Fori(0, NGROUP - 1) as g:
                attention("loop", g)
                spread_w("loop", g, g * 2 + 1, 1, False)
                store_w("loop", g, "ffn1", g * 2 + 2, 0)
                spread_w("loop", g, g * 2 + 2, 0, True)
                for q in range(4):
                    store_e("loop", g, "qkv", g + 1, q)
                    if q:
                        load_band("loop", g, g + 1, q - 1)
                load_band("loop", g, g + 1, 3)
                store_x(g)
            last = NGROUP - 1
            attention("last", last)
            store_w("last", last, "ffn1", 2 * last + 1, 1)
            spread_w("last", last, 2 * last + 1, 1, False)
            store_x(last)
            sp.wait_ge(stored, 16 + 16 * NGROUP)
            for s in skew_stored:
                sp.wait_ge(s, 8 * NQ * NGROUP)
            sp.wait_ge(wd_stored, 16 * 2 * NGROUP)

        @block.gpsimd
        def _(pool):
            def affine(tile, pattern, base, channel, fill, op):
                return nc.gpsimd.affine_select(out=tile, in_=tile, compare_op=op, fill=fill, base=base,
                                               pattern=pattern, channel_multiplier=channel)

            nc.gpsimd.memset(raw_bias[:, :], 0.0).then_inc(zeroed, 1)
            nc.gpsimd.memset(ident[:, :], 0.0).then_inc(const_ready, 1)
            nc.gpsimd.memset(tri[:, :, :], 1.0).then_inc(const_ready, 1)
            nc.gpsimd.memset(mask, 0.0).then_inc(const_ready, 1)
            nc.gpsimd.memset(epst[:, :], EPS).then_inc(const_ready, 1)
            nc.gpsimd.memset(mhalf[:, :], -0.5).then_inc(const_ready, 1)
            pool.wait_ge(const_ready, 5)
            affine(ident[:, :], [[-1, P]], 0, 1, 1.0, ALU.not_equal).then_inc(const_ready, 1)
            affine(tri[:, :, :], [[1, E], [-1, E]], -1, 0, 0.0, ALU.is_ge).then_inc(const_ready, 1)
            affine(mask, [[1, P]], -(P - 1), 1, NEG, ALU.is_ge).then_inc(const_ready, 1)
            nc.gpsimd.memset(raw_r, 0.0).then_inc(zeroed, 1)
            nc.gpsimd.memset(raw_b, 0.0).then_inc(zeroed, 1)

            def rstd_of(n):
                pool.wait_ge(mv_ready, n + 1)
                nc.gpsimd.tensor_tensor(var[:, :], mv[:, :, 1], epst[:, :], ALU.add).then_inc(var_ready, 1)
                pool.wait_ge(var_ready, n + 1)
                nc.gpsimd.tensor_tensor(rstd[:, :], var[:, :], mhalf[:, :], ALU.pow).then_inc(rstd_ready, 1)

            def ffn(where, g, f, second, hooks):
                for c in range(NCH):
                    for hook in hooks.get(c, []):
                        hook()
                    if c == 0 and where == "loop" and not second:
                        pool.wait_ge(pn_ready, (g + 1) * NP)
                    if c in (0, 2) and where != "loop":
                        pool.wait_ge(wide_full[0], weight_uses(where, g, second) * 16 + (8 if c == 0 else 16))
                    elif c % 4 == 0:
                        pool.wait_ge(wide_full[c // 4], weight_uses(where, g, second) * 16 + 16)
                    if not (where == "pro" and c < 4):
                        pool.wait_ge(h_ready, f * NCH + c - 3)
                    pool.wait_ge(sg_ready, f * NCH + c + 1)
                    wb = wide[:, c // 4, 512 * (c // 2 % 2):512 * (c // 2 % 2) + 512]
                    nc.gpsimd.tensor_tensor(sw_s[c % 4], sg_s[c % 4], wb, ALU.mult).then_inc(sw_ready, 1)

            def attention(where, g):
                for p in range(NP):
                    if p == 4 and where == "loop":
                        rstd_of(g * 3 + 2)
                    if p >= 4:
                        pool.wait_ge(pt_full, g * NP + p - 3)
                    pool.wait_ge(rc_ready, g * NP + p + 1)
                    ri = rsum[:, 2 * p:2 * p + 2].unsqueeze(2).to_broadcast([P, 2, 256])
                    nc.gpsimd.tensor_tensor(pn_s[p % 4].rearrange("p (h c) -> p h c", h=2),
                                            ex_s[p % 4].rearrange("p (h c) -> p h c", h=2),
                                            ri, ALU.mult).then_inc(pn_ready, 1)

            rstd_of(0)
            def split(i):
                if not on_pool(order[i]):
                    return
                pool.wait_ge(split_hi, i + 1)
                raw, hi, lo = pieces[i]
                nc.gpsimd.tensor_tensor(lo, raw, hi.bitcast(F32), ALU.subtract).then_inc(split_lo_pool, 1)

            ffn("pro", 0, 0, False, {c + 1: [lambda i=i: split(i) for i in split_at[c]] for c in range(NCH - 1)})
            for i in split_at[NCH - 1]:
                split(i)
            nc.gpsimd.memset(negs, NEG).then_inc(negs_ready, 1)
            rstd_of(1)
            pool.wait_ge(split_lo, split_count("b"))
            pool.wait_ge(s_neg, 48)
            pool.wait_ge(stored, 16)
            pool.wait_ge(misc_done, 1)
            nc.gpsimd.memset(kt[:, :, 0:P], 0.0).then_inc(kv_zeroed, 1)
            nc.gpsimd.memset(vt[:, 0, :], 0.0).then_inc(kv_zeroed, 1)
            with pool.Fori(0, NGROUP - 1) as g:
                attention("loop", g)
                ffn("loop", g, g * 2 + 1, False, {3: [lambda: rstd_of(g * 3 + 3)]})
                ffn("loop", g, g * 2 + 2, True, {3: [lambda: rstd_of(g * 3 + 4)]})
            last = NGROUP - 1
            attention("last", last)
            rstd_of(3 * last + 2)
            ffn("last", last, 2 * last + 1, False, {})

        @block.scalar
        def _(act):
            def split(i, loaded):
                for s, n in loaded:
                    act.wait_ge(s, n)
                raw, hi, _ = pieces[i]
                nc.scalar.activation(hi, raw, ACT.Copy).then_inc(split_hi, 1)

            def x_hi(where, g, stage, buf):
                act.wait_ge(misc_full, misc_use(where, g, stage, "x") + 1)
                nc.scalar.activation(xh[buf][:, :], misc[:, :], ACT.Copy).then_inc(xh_ready, 1)

            def route_exp(f):
                act.wait_ge(rt_link, f * RT + 3)
                nc.scalar.activation(ex[:, :, :], dl[:, :, :], ACT.Exp).then_inc(ex_ready, 1)

            def w_out(where, g, stage, f):
                if where != "pro":
                    act.wait_ge(wd_stored, f * 16)
                act.wait_ge(misc_full, misc_use(where, g, stage, "w") + 1)
                nc.scalar.activation(w_t[:, :], misc[0:E, :], ACT.Copy).then_inc(misc_done, 1)

            def z_out(where, g):
                act.wait_ge(z_full, g + 1)
                nc.scalar.activation(yz, (acc if where == "loop" else bank[0])[:, :], ACT.Identity, bias=bias[:, BP:BP + 1]).then_inc(z_done, 1)

            def hidden_hi(f, c):
                act.wait_ge(h_ready, f * NCH + c + 1)
                if c >= 4:
                    act.wait_ge(h_used, f * (NCH - 1) + c - 3)
                nc.scalar.activation(rs[:, c % 4, :], hd_s[c % 4], ACT.Copy).then_inc(hh_ready, 1)

            def ffn(where, f, hooks, chunks=range(NCH), then=None, his=0):
                for c in chunks:
                    for hook in hooks.get(c, []):
                        hook()
                    if not (where == "pro" and c < 4):
                        act.wait_ge(sw_ready, f * NCH + c - 3)
                    act.wait_ge(g_full, f * NCH + c + 1)
                    nc.scalar.activation(sg_s[c % 4], bank[c % 2][:, :], ACT.Silu,
                                         bias=bias[:, BG + c:BG + c + 1]).then_inc(sg_ready, 1)
                    if chunks[-1] == NCH - 1:
                        for k in range(his if c == chunks[0] else max(0, c - 2), c - 1):
                            hidden_hi(f, k)
                if chunks[-1] != NCH - 1:
                    return
                hidden_hi(f, NCH - 2)
                hidden_hi(f, NCH - 1)
                if then is not None:
                    then()
                act.wait_ge(y_full, f + 1)
                nc.scalar.activation(yz, acc[:, :], ACT.Copy, scale=0.5).then_inc(y_done, 1)

            def e_out(where, g, stage, gq, q):
                act.wait_ge(skew_stored[q % 2], gq * (8 * NQ) + 16 * (q // 2))
                act.wait_ge(misc_full, misc_use(where, g, stage, f"e{q}") + 1)
                nc.scalar.activation(es[:, q % 2, :], misc[:, :], ACT.Copy).then_inc(misc_done, 1)

            def qkv(where, g, gq):
                n = 0
                for i in range(NQK):
                    if i % 4 < 2:
                        act.wait_ge(qkv_full[0], gq * (NQK // 2) + n + 1)
                        src, n = bank[i % 4][:, :], n + 1
                        if i < 8:
                            nc.scalar.activation(qt[:, i, :], src, ACT.Identity, scale=0.125,
                                                 bias=bias[:, BQ + i:BQ + i + 1]).then_inc(qkv_done[0], 1)
                        else:
                            nc.scalar.activation(kt[:, i - 8, P:], src, ACT.Copy).then_inc(qkv_done[0], 1)
                    if i in (0, 2, 4, 6):
                        q = i // 2
                        act.wait_ge(rs_full, gq * 4 + q + 1)
                        nc.scalar.activation(rs[:, q, :], ptb[q % 2][:, :], ACT.Identity,
                                             bias=bias[:, BR + q:BR + q + 1]).then_inc(rs_hi, 1)
                    if i in E_AFTER and where != "pro":
                        e_out(where, g, "qkv", gq, E_AFTER.index(i))

            def v_out(g, j):
                act.wait_ge(v_full[0], g * (NV // 2) + v_count(j))
                c = 512 * (j % 2)
                nc.scalar.activation(vt[:, 1 + j // 2, c:c + 512], v_bank[j % 3][:, :], ACT.Copy).then_inc(v_done[0], 1)

            def attention(where, g):
                for s in range(NQ + LAG):
                    if s == X_STEP + 1 and where == "loop":
                        x_hi(where, g, "att", 0)
                    if s == W_STEP + 1 and where == "loop":
                        w_out(where, g, "att", g * 2 + 1)
                    if s >= NQ and where == "loop":
                        if s == NQ:
                            act.wait_ge(p_ready, (g + 1) * NH)
                        ffn(where, g * 2 + 1, {}, range(s - NQ, s - NQ + 1))
                    if s < NQ:
                        if s == 0:
                            nc.scalar.activation(warm[:, :], epst[:, 0:1], ACT.Exp)
                            e_out(where, g, "att", g, 4)
                            v_out(g, 0)
                        late = where == "loop" and s in E_LATE
                        if LAG <= s < NQ - 4 and not late:
                            e_out(where, g, "att", g, s + 4)
                        for i in range(4):
                            if (s, i) in ((0, 2), (1, 1), (1, 3)):
                                v_out(g, 3 if s == 0 else 4 if i == 1 else 7)
                            n = 4 * s + i
                            if i % 2 == 0 and n >= 8:
                                act.wait_ge(pn_ready, g * NP + n // 2 - 3)
                            act.wait_ge(l_ready, g * NH + n + 1)
                            nc.scalar.activation(ex_s[n // 2 % 4][:, 256 * (i % 2):256 * (i % 2) + 256], lg_s[i],
                                                 ACT.Exp, bias=nmx[:, n:n + 1], scale=-1.0,
                                                 accum_out=sums[:, n:n + 1]).then_inc(p_ready, 1)
                            if (s == 1 and i == 1) or (late and i == 0):
                                e_out(where, g, "att", g, s + 4)
                    if s == ROUTE_STEP + 1 and where == "loop":
                        route_exp(g * 2 + 1)
                    if s >= LAG and (s - LAG) % 2 == 1:
                        u = (s - LAG) // 2
                        act.wait_ge(av_full, g * NP + 4 * u + 4)
                        nc.scalar.activation(qt[:, 4 * (u % 2):4 * (u % 2) + 4, P * (u // 2):P * (u // 2) + P],
                                             acc[:, :].rearrange("p (a t) -> p a t", a=4),
                                             ACT.Copy).then_inc(av_done, 1)
                if where == "loop":
                    ffn(where, g * 2 + 1, {}, range(2, 3))
                    hidden_hi(g * 2 + 1, 0)
                    hidden_hi(g * 2 + 1, 1)
                z_out(where, g)

            act.wait_ge(misc_full, 1)
            nc.scalar.activation(bias[:, 0:NBIAS], misc[:, 0:NBIAS], ACT.Copy).then_inc(misc_done, 1)
            split(0, [(s_rt, 16)])
            x_hi("pro", 0, "route", 0)
            split(1, [(s_gu[0], 32)])
            split(2, [(s_gu[1], 32)])
            route_exp(0)
            ffn("pro", 0, {}, range(2))
            w_out("pro", 0, "route", 0)
            loads = {"r": [(s_wr, 16 * len(STACK))],
                     "b": [(s_brev, 16 * sum(len(stacked_heads(c0, c1)) for _, c0, c1 in STACK))]}
            loads.update({f"gu{e}": [(s_gu[e], 32)] for e in range(E)})
            loads.update({f"wo{i}": [(s_wo, 16)] for i in range(4)})
            loads.update({f"qkv{i}": [(s_qkv[i // 2], 16)] for i in range(6)})
            hooks = {c + 1: [lambda i=i: split(i, loads[order[i]]) for i in split_at[c]] for c in range(2, NCH - 1)}
            hooks[2] = [lambda i=i: split(i, loads[order[i]]) for i in (*split_at[0], *split_at[1])]
            hooks[NCH - 1] += [lambda i=i: split(i, loads[order[i]]) for i in split_at[NCH - 1]]
            ffn("pro", 0, hooks, range(2, NCH))
            x_hi("pro", 0, "ffn2", 0)
            act.wait_ge(kv_zeroed, 2)
            act.wait_ge(bq_scaled, 1)
            qkv("pro", 0, 0)
            with act.Fori(0, NGROUP - 1) as g:
                attention("loop", g)

                def carry(to, of):
                    nc.scalar.activation(to, of, ACT.Copy).then_inc(carried, 1)

                ffn("loop", g * 2 + 1, {4: [lambda: carry(kt[:, :, 0:P], kt[:, :, GT:GT + P])],
                                        6: [lambda: carry(vt[:, 0, :], vt[:, NBLK, :])],
                                        8: [lambda: x_hi("loop", g, "ffn1", 1)],
                                        10: [lambda: route_exp(g * 2 + 2)],
                                        15: [lambda: w_out("loop", g, "ffn1", g * 2 + 2)]}, range(3, NCH),
                    lambda: ffn("loop", g * 2 + 2, {}, range(2)), 2)
                ffn("loop", g * 2 + 2, {7: [lambda: x_hi("loop", g, "ffn2", 0)]}, range(2, NCH))
                act.wait_ge(carried, g * 2 + 2)
                qkv("loop", g, g + 1)
            last = NGROUP - 1
            attention("last", last)
            x_hi("last", last, "ffn1", 1)
            route_exp(2 * last + 1)
            ffn("last", 2 * last + 1, {}, range(2))
            w_out("last", last, "ffn1", 2 * last + 1)
            ffn("last", 2 * last + 1, {}, range(2, NCH))

        @block.vector
        def _(dve):
            v = nc.vector

            def split(i):
                if on_pool(order[i]):
                    return
                dve.wait_ge(split_hi, i + 1)
                rows = slice(0, NR if order[i] == "b" else P)
                raw, hi, lo = (ap[rows, :] for ap in pieces[i])
                v.tensor_tensor(lo, raw, hi.bitcast(F32), ALU.subtract).then_inc(split_lo, 1)

            def stats(n, x):
                for t in range(NBLK):
                    ins = v.bn_stats(st[:, t, :], x[:, t, :])
                ins.then_inc(stats_done, 1)
                dve.wait_ge(stats_done, n + 1)
                v.memset(gate[:, 2:3], 0.0)
                for t in range(NBLK):
                    ins = v.bn_aggr(mv[:, t, :], st[:, t, :])
                ins.then_inc(mv_ready, 1)

            def normalise(n, x):
                dve.wait_ge(rstd_ready, n + 1)
                for t in range(NBLK):
                    ins = v.tensor_scalar(xn[:, t, :], x[:, t, :], mv[:, t, 0:1], rstd[:, t:t + 1],
                                          ALU.subtract, ALU.mult)
                ins.then_inc(xn_ready, 1)

            def x_lo(where, g, stage, n, buf):
                dve.wait_ge(xh_ready, n + 1)
                v.tensor_tensor(xl[buf][:, :], misc[:, :], xh[buf][:, :].bitcast(F32), ALU.subtract).then_inc(misc_done, 1)

            def residual(where, g, stage, use, new, old):
                dve.wait_ge(misc_full, misc_use(where, g, stage, use) + 1)
                v.tensor_tensor(new[:, :, :], misc[:, :].rearrange("p (t d) -> p t d", t=NBLK), old[:, :, :],
                                ALU.add).then_inc(misc_done, 1)
                dve.wait_ge(misc_done, misc_use(where, g, stage, use) + 1)

            def per_token(t):
                return t[:, :].unsqueeze(2).to_broadcast([P, NBLK, E])

            def route_a(where, g, stage, f):
                dve.wait_ge(misc_full, misc_use(where, g, stage, "route") + 1)
                v.tensor_copy(lg[:, :, :], misc[:, 0:NBLK * E].rearrange("p (t e) -> p t e", t=NBLK)).then_inc(misc_done, 1)
                dve.wait_ge(misc_done, misc_use(where, g, stage, "route") + 1)
                v.tensor_reduce(mx[:, :], lg[:, :, :], X, ALU.max).then_inc(rt_link, 1)
                dve.wait_ge(rt_link, f * RT + 1)
                v.tensor_tensor(dl[:, :, :], lg[:, :, :], per_token(mx), ALU.subtract).then_inc(rt_link, 2)

            def route_b(f, links=range(3, RT)):
                other = ex[:, :, :].unsqueeze(2).to_broadcast([P, NBLK, E, E])
                own = ex[:, :, :].unsqueeze(3).to_broadcast([P, NBLK, E, E])
                lower = tri[:, :, :].unsqueeze(1).to_broadcast([P, NBLK, E, E])
                step = {
                    3: lambda: v.tensor_reduce(se[:, :], ex[:, :, :], X, ALU.add),
                    4: lambda: v.tensor_tensor(gt[:, :, :, :], other, own, ALU.is_gt),
                    5: lambda: v.tensor_tensor(eq[:, :, :, :], other, own, ALU.is_equal),
                    6: lambda: v.tensor_tensor(eq[:, :, :, :], eq[:, :, :, :], lower, ALU.mult),
                    7: lambda: v.tensor_tensor(gt[:, :, :, :], gt[:, :, :, :], eq[:, :, :, :], ALU.add),
                    8: lambda: v.tensor_reduce(rank[:, :, :], gt[:, :, :, :], X, ALU.add),
                    9: lambda: v.scalar_tensor_tensor(ew[:, :, :], rank[:, :, :], 1.5, ex[:, :, :], ALU.is_lt, ALU.mult),
                    10: lambda: v.tensor_reduce(s2[:, :], ew[:, :, :], X, ALU.add),
                    11: lambda: v.scalar_tensor_tensor(den[:, :], se[:, :], 1.0e-8, s2[:, :], ALU.mult, ALU.add),
                    12: lambda: v.reciprocal(rden[:, :], den[:, :]),
                    13: lambda: v.tensor_tensor(w[:, :, :], ew[:, :, :], per_token(rden), ALU.mult),
                }
                for n in links:
                    if n == 3:
                        dve.wait_ge(ex_ready, f + 1)
                    else:
                        dve.wait_ge(rt_link, f * RT + n)
                    step[n]().then_inc(rt_link, 1)

            def w_wide(where, g, stage, e):
                dve.wait_ge(misc_full, misc_use(where, g, stage, f"b{e}") + 1)
                v.tensor_copy(wide[:, 0, GT * e:GT * e + GT], misc[:, :]).then_inc(misc_done, 1)
                v.memset(gate[:, 3 + e:4 + e], 0.0).then_inc(wide_full[0], 8)

            def hidden_lo(where, f, c):
                if c >= 3:
                    dve.wait_ge(h_used, f * (NCH - 1) + c - 2)
                elif where != "pro":
                    dve.wait_ge(y_full, f)
                dve.wait_ge(hh_ready, f * NCH + c + 1)
                v.tensor_tensor(hid_lo[:, c % 3, :], hd_s[c % 4], rs[:, c % 4, :].bitcast(F32),
                                ALU.subtract).then_inc(hl_ready, 1)

            def ffn(where, f, hooks):
                for c in range(NCH):
                    for hook in hooks.get(c, []):
                        hook()
                    if not (where == "pro" and c < 4):
                        dve.wait_ge(hl_ready, f * NCH + c - 3)
                    dve.wait_ge(u_full, f * NCH + c + 1)
                    dve.wait_ge(sw_ready, f * NCH + c + 1)
                    v.scalar_tensor_tensor(hd_s[c % 4], up_bank[c % 4][:, :], bias[:, BU + c:BU + c + 1],
                                           sw_s[c % 4], ALU.add, ALU.mult).then_inc(h_ready, 1)
                    if c >= 2:
                        hidden_lo(where, f, c - 2)
                hidden_lo(where, f, NCH - 2)
                hidden_lo(where, f, NCH - 1)

            def qkv(where, g, gq):
                n = 0
                for i in range(NQK):
                    if i % 4 >= 2:
                        dve.wait_ge(qkv_full[1], gq * (NQK // 2) + n + 1)
                        src, n = bank[i % 4][:, :], n + 1
                        if i < 8:
                            v.tensor_scalar(qt[:, i, :], src, 0.125, bias[:, BQ + i:BQ + i + 1],
                                            ALU.mult, ALU.add).then_inc(qkv_done[1], 1)
                        else:
                            v.tensor_copy(kt[:, i - 8, P:], src).then_inc(qkv_done[1], 1)
                    if i in (0, 2, 4, 6):
                        q = i // 2
                        rows = slice(64, 64 + NR)
                        dve.wait_ge(rs_hi, gq * 4 + q + 1)
                        v.scalar_tensor_tensor(rs[rows, q, :], ptb[q % 2][rows, :], bias[rows, BR + q:BR + q + 1],
                                               rs[rows, q, :].bitcast(F32), ALU.add, ALU.subtract).then_inc(rs_lo, 1)
                    if i == 3 and where == "loop":
                        residual(where, g, "qkv", "y", x2, x2)
                        v.memset(gate[:, 1:2], 0.0).then_inc(x3_done, 1)
                    if i in E_AFTER and where == "pro":
                        q = E_AFTER.index(i)
                        if q >= 2:
                            dve.wait_ge(skew_stored[q % 2], 16 * (q // 2))
                        dve.wait_ge(misc_full, misc_use(where, g, "qkv", f"e{q}") + 1)
                        v.tensor_tensor(es[:, q % 2, :].rearrange("p (h j) -> p h j", h=4),
                                        misc[:, :].rearrange("p (h j) -> p h j", h=4),
                                        mask.unsqueeze(1).to_broadcast([P, 4, P]), ALU.add).then_inc(misc_done, 1)

            def v_out(g, j):
                dve.wait_ge(v_full[1], g * (NV // 2) + v_count(j))
                c = 512 * (j % 2)
                v.tensor_copy(vt[:, 1 + j // 2, c:c + 512], v_bank[j % 3][:, :]).then_inc(v_done[1], 1)

            def pt_out(g, p):
                if p >= 2:
                    dve.wait_ge(av_full, g * NP + p - 1)
                dve.wait_ge(pt_full, g * NP + p + 1)
                v.tensor_copy(pt_s[p % 2], ptb[p % 2][:, :]).then_inc(pt_done, 1)

            def recip(g, p):
                dve.wait_ge(p_ready, g * NH + 2 * p + 2)
                v.reciprocal(rsum[:, 2 * p:2 * p + 2], sums[:, 2 * p:2 * p + 2]).then_inc(rc_ready, 1)

            def attention(where, g):
                for s in range(NQ + LAG):
                    if s >= LAG:
                        pt_out(g, 2 * (s - LAG))
                    if 1 <= s <= NQ:
                        recip(g, 2 * s - 1)
                    if s >= LAG:
                        pt_out(g, 2 * (s - LAG) + 1)
                    if where == "loop":
                        if s == X_STEP + 1:
                            x_lo(where, g, "att", g * 3 + 2, 0)
                        if s == ROUTE_STEP + 1:
                            route_a(where, g, "att", g * 2 + 1)
                    if s < NQ:
                        dve.wait_ge(s_full, g * NQ + s + 1)
                        dve.wait_ge(wide_full[s % 4], band_uses(g, s) * 16 + 16)
                        if s:
                            dve.wait_ge(p_ready, g * NH + 4 * s)
                        v.memset(gate[:, 0:1], 0.0)
                        for i in range(4):
                            n = 4 * s + i
                            v.tensor_tensor_reduce(out=lg_s[i],
                                                   in0=bank[2 * (s % 2) + i % 2][:, 256 * (i // 2):256 * (i // 2) + 256],
                                                   in1=wide[:, s % 4, 256 * i:256 * i + 256],
                                                   scale=-1.0, scalar=3.0e38, op0=ALU.add, op1=ALU.min,
                                                   accum_out=nmx[:, n:n + 1]).then_inc(l_ready, 1)
                        if s < 2:
                            v_out(g, (1, 5)[s])
                        recip(g, 2 * s)
                        if s < 2:
                            v_out(g, (2, 6)[s])
                        if where == "loop" and s == 1:
                            dve.wait_ge(s_x, g * 16 + 32)
                            stats(g * 3 + 2, x0)
                        if where == "loop" and s == 3:
                            normalise(g * 3 + 2, x0)
                        if where == "loop" and ROUTE_STEP < s < W_STEP:
                            first = (3, 5, 7, 8, 10, RT)
                            route_b(g * 2 + 1, range(first[s - ROUTE_STEP - 1], first[s - ROUTE_STEP]))

            dve.wait_ge(s_x, 16)
            stats(0, x0)
            normalise(0, x0)
            split(0)
            dve.wait_ge(misc_done, 1)
            v.tensor_scalar(bias[:, BQ:BP], bias[:, BQ:BP], 0.125, None, ALU.mult).then_inc(bq_scaled, 1)
            x_lo("pro", 0, "route", 0, 0)
            split(1)
            split(2)
            route_a("pro", 0, "route", 0)
            route_b(0)
            w_wide("pro", 0, "route", 0)
            w_wide("pro", 0, "route", 1)
            ffn("pro", 0, {c: [lambda i=i: split(i) for i in split_at[c]] for c in range(NCH)})
            residual("pro", 0, "ffn2", "y", x1, x0)
            v.memset(gate[:, 1:2], 0.0).then_inc(x1_done, 1)
            stats(1, x1)
            normalise(1, x1)
            x_lo("pro", 0, "ffn2", 1, 0)
            dve.wait_ge(kv_zeroed, 2)
            dve.wait_ge(bq_scaled, 1)
            qkv("pro", 0, 0)
            with dve.Fori(0, NGROUP - 1) as g:
                attention("loop", g)

                def tail2():
                    dve.wait_ge(stored, g * 16 + 16)
                    residual("loop", g, "ffn1", "z", x2, x1)
                    stats(g * 3 + 3, x2)

                def tail1():
                    residual("loop", g, "ffn2", "y", x1, x0)
                    v.memset(gate[:, 1:2], 0.0).then_inc(x1_done, 1)
                    stats(g * 3 + 4, x1)

                ffn("loop", g * 2 + 1, {2: [tail2], 4: [lambda: normalise(g * 3 + 3, x2)],
                                        7: [lambda: x_lo("loop", g, "ffn1", g * 3 + 3, 1)],
                                        9: [lambda: route_a("loop", g, "ffn1", g * 2 + 2)],
                                        10: [lambda: route_b(g * 2 + 2, range(3, 6))],
                                        11: [lambda: route_b(g * 2 + 2, range(6, 9))],
                                        12: [lambda: route_b(g * 2 + 2, range(9, RT))]})
                ffn("loop", g * 2 + 2, {2: [tail1], 4: [lambda: normalise(g * 3 + 4, x1)],
                                        6: [lambda: x_lo("loop", g, "ffn2", g * 3 + 4, 0)]})
                dve.wait_ge(carried, g * 2 + 2)
                qkv("loop", g, g + 1)
            last = NGROUP - 1
            attention("last", last)
            dve.wait_ge(stored, last * 16 + 16)
            residual("last", last, "ffn1", "z", x2, x1)
            stats(3 * last + 2, x2)
            normalise(3 * last + 2, x2)
            x_lo("last", last, "ffn1", 3 * last + 2, 1)
            route_a("last", last, "ffn1", 2 * last + 1)
            route_b(2 * last + 1)
            dve.wait_ge(l_ready, last * NH + NH)
            w_wide("last", last, "ffn1", 0)
            w_wide("last", last, "ffn1", 1)
            ffn("last", 2 * last + 1, {})
            residual("last", last, "end", "y", x2, x2)
            v.memset(gate[:, 1:2], 0.0).then_inc(x3_done, 1)

        @block.tensor
        def _(pe):
            mm = nc.tensor.matmul

            def three(out_ap, w_hi, w_lo, m_hi, m_lo):
                mm(out_ap, w_hi, m_hi, start=True, stop=False)
                mm(out_ap, w_lo, m_hi, start=False, stop=False)
                return mm(out_ap, w_hi, m_lo, start=False, stop=True)

            def claim(where, g, stage, use):
                n = misc_use(where, g, stage, use)
                if not (where == "pro" and n == 0):
                    pe.wait_ge(misc_done, n)

            def turn(src):
                for t in range(NBLK):
                    ins = nc.tensor.transpose(misc[:, P * t:P * t + P], src(t), ident[:, :])
                ins.then_inc(misc_full, 1)

            def x_turn(where, g, stage, n):
                claim(where, g, stage, "x")
                pe.wait_ge(xn_ready, n + 1)
                turn(lambda t: xn[:, t, :])

            def back(where, g, stage, use, s, count):
                claim(where, g, stage, use)
                pe.wait_ge(s, count)
                turn(lambda t: yz[:, P * t:P * t + P])

            def route(where, g, stage, buf):
                claim(where, g, stage, "route")
                for t in range(NBLK):
                    xt = slice(P * t, P * t + P)
                    o = misc[:, E * t:E * t + E]
                    mm(o, xh[buf][:, xt], rt_hi[:, :], start=True, stop=False)
                    mm(o, xl[buf][:, xt], rt_hi[:, :], start=False, stop=False)
                    ins = mm(o, xh[buf][:, xt], rt_lo[:, :], start=False, stop=True)
                ins.then_inc(misc_full, 1)

            def w_turn(where, g, stage, f):
                claim(where, g, stage, "w")
                pe.wait_ge(rt_link, f * RT + RT)
                for t in range(NBLK):
                    ins = nc.tensor.transpose(misc[0:E, P * t:P * t + P], w[:, t, :], ident[:, :])
                ins.then_inc(misc_full, 1)

            def w_wide(where, g, stage, e):
                claim(where, g, stage, f"b{e}")
                mm(misc[:, :], ident[0:E, e:e + 1].to_broadcast([E, P]), w_t[:, :], start=True, stop=True).then_inc(misc_full, 1)

            def ffn(where, f, buf, x_use, w_use, acc_free, hooks, chunks=range(NCH + DLAG), up_free=None):
                for c in chunks:
                    for hook in hooks.get(c, []):
                        hook()
                    if c < NCH:
                        e, m = c // 2, P * (c % 2)
                        if c == 0:
                            pe.wait_ge(misc_done, x_use + 1)
                        if where == "pro" and c % 2 == 0:
                            pe.wait_ge(split_lo, split_count(f"gu{e}"))
                        if not (where == "pro" and c < 2):
                            pe.wait_ge(sg_ready, f * NCH + c - 1)
                        three(bank[c % 2][:, :], gu_hi[:, e, 0, m:m + P], gu_lo[:, e, 0, m:m + P],
                              xh[buf][:, :], xl[buf][:, :]).then_inc(g_full, 1)
                        if up_free is not None:
                            pe.wait_ge(*up_free)
                        elif not (where == "pro" and c < 4):
                            pe.wait_ge(h_ready, f * NCH + c - 3)
                        three(up_bank[c % 4][:, :], gu_hi[:, e, 1, m:m + P], gu_lo[:, e, 1, m:m + P],
                              xh[buf][:, :], xl[buf][:, :]).then_inc(u_full, 1)
                    if c == DLAG:
                        for hook in hooks.get("open", []):
                            hook()
                        pe.wait_ge(misc_done, w_use + 1)
                        if acc_free:
                            pe.wait_ge(*acc_free)
                        if where == "pro":
                            pe.wait_ge(s_bo, 16)
                        mm(acc[:, :], bo_s[:, :], w_t[:, :], start=True, stop=False)
                    if c >= DLAG:
                        k = c - DLAG
                        if where == "pro" and k % 4 == 0:
                            pe.wait_ge(split_lo, split_count(f"wo{k // 4}"))
                        pe.wait_ge(hl_ready, f * NCH + k + 1)
                        mm(acc[:, :], wo_hi[:, k, :], rs[:, k % 4, :], start=False, stop=False)
                        mm(acc[:, :], wo_lo[:, k, :], rs[:, k % 4, :], start=False, stop=False)
                        ins = mm(acc[:, :], wo_hi[:, k, :], hid_lo[:, k % 3, :], start=False, stop=(k == NCH - 1))
                        ins.then_inc(y_full if k == NCH - 1 else h_used, 1)

            def e_mm(where, g, stage, q):
                claim(where, g, stage, f"e{q}")
                blk = slice(P * (q // 4), P * (q // 4) + P)
                mm(misc[:, :], rs[:, q % 4, blk], b_mix[:, :], start=True, stop=True).then_inc(misc_full, 1)

            def qkv(where, g, gq, f, outputs=range(NQK)):
                if where == "pro":
                    pe.wait_ge(split_lo, split_count("b"))
                    pe.wait_ge(split_lo_pool, split_count("qkv5"))
                for i in outputs:
                    side = i % 4 // 2
                    if i >= 4:
                        pe.wait_ge(qkv_done[side], gq * (NQK // 2) + i // 4 * 2 + i % 2 - 1)
                    a, c = i // 8, P * (i % 8)
                    three(bank[i % 4][:, :], qkv_hi[:, a, c:c + P], qkv_lo[:, a, c:c + P],
                          xh[0][:, :], xl[0][:, :]).then_inc(qkv_full[side], 1)
                    if i in (0, 2, 4, 6):
                        q = i // 2
                        if q >= 2:
                            pe.wait_ge(rs_lo, gq * 4 + q - 1)
                        three(ptb[q % 2][:, :], r_hi[:, q, :], r_lo[:, q, :], xh[0][:, :], xl[0][:, :]).then_inc(rs_full, 1)
                    if i == 3 and where == "loop":
                        back(where, g, "qkv", "y", y_done, f + 1)
                    if i in E_AFTER:
                        if i == E_AFTER[0]:
                            pe.wait_ge(rs_lo, gq * 4 + 4)
                        e_mm(where, g, "qkv", E_AFTER.index(i))

            def values(g, j):
                if j >= 3:
                    pe.wait_ge(v_done[V_SIDE[j - 3]], g * (NV // 2) + v_count(j - 3))
                elif j == 2:
                    pe.wait_ge(y_done, g * 2 + 1)
                else:
                    pe.wait_ge(rs_lo, g * 4 + 4)
                t, c = P * (j // 2), 512 * (j % 2)
                three(v_bank[j % 3][:, :], xh[0][:, t:t + P], xl[0][:, t:t + P],
                      qkv_hi[:, 2, c:c + 512], qkv_lo[:, 2, c:c + 512]).then_inc(v_full[V_SIDE[j]], 1)

            def scores(g, s):
                b = s // 4
                if s >= 2:
                    pe.wait_ge(l_ready, g * NH + 4 * (s - 1))
                for jj in range(2):
                    j = 2 * (s % 4) + jj
                    for hh in range(2):
                        r = slice(64 * hh, 64 * hh + 64)
                        ins = mm(bank[2 * (s % 2) + hh][:, 256 * jj:256 * jj + 256], qt[r, j, P * b:P * b + P],
                                 kt[r, j, P * b:P * b + 2 * P], start=True, stop=True)
                ins.then_inc(s_full, 1)

            def pt(g, p):
                pe.wait_ge(pn_ready, g * NP + p + 1)
                if p >= 2:
                    pe.wait_ge(pt_done, g * NP + p - 1)
                for k in range(4):
                    ins = nc.tensor.transpose(ptb[p % 2][:, P * k:P * k + P], pn_s[p % 4][:, P * k:P * k + P], ident[:, :])
                ins.then_inc(pt_full, 1)

            def av(g, p):
                b, j = p // 8, p % 8
                if p % 4 == 0 and p:
                    pe.wait_ge(av_done, g * (NP // 4) + p // 4)
                pe.wait_ge(pt_done, g * NP + p + 1)
                for k in range(2):
                    for hh in range(2):
                        ins = mm(acc[64 * hh:64 * hh + 64, P * (p % 4):P * (p % 4) + P],
                                 vt[:, b + k, P * j + 64 * hh:P * j + 64 * hh + 64],
                                 pt_s[p % 2][:, 256 * hh + P * k:256 * hh + P * k + P], start=(k == 0), stop=(k == 1))
                ins.then_inc(av_full, 1)

            def project(to, c0, c1):
                for j in range(NPAIR):
                    ins = mm(to[:, c0:c1], wp_s[:, j, :], qt[:, j, c0:c1], start=(j == 0), stop=(j == NPAIR - 1))
                return ins

            def attention(where, g):
                def next_ffn(c):
                    ffn(where, g * 2 + 1, 0, misc_use(where, g, "att", "x"), misc_use(where, g, "att", "w"),
                        None, {}, range(c, c + 1), (l_ready, (g + 1) * NH) if c < 2 else (pt_done, (g + 1) * NP))

                pe.wait_ge(qkv_done[0], (g + 1) * (NQK // 2))
                pe.wait_ge(qkv_done[1], g * (NQK // 2) + NQK // 4)
                for s in range(NQ + LAG):
                    if s == 1:
                        pe.wait_ge(qkv_done[1], (g + 1) * (NQK // 2))
                    p0 = 2 * (s - LAG)
                    if s >= LAG:
                        if s == LAG:
                            pe.wait_ge(v_done[V_SIDE[6]], (g + 1) * (NV // 2))
                        pt(g, p0)
                        if s == LAG:
                            pe.wait_ge(v_done[V_SIDE[7]], (g + 1) * (NV // 2))
                        pt(g, p0 + 1)
                    late = where == "loop" and s in E_LATE
                    if LAG <= s < NQ - 4 and not late:
                        e_mm(where, g, "att", s + 4)
                    if s >= NQ and where == "loop":
                        next_ffn(s - NQ)
                    if s >= NQ and where == "last":
                        if s == NQ:
                            pe.wait_ge(l_ready, (g + 1) * NH)
                        done = (0, NBLK - 2, NBLK - 1)[s - NQ:s - NQ + 2]
                        pe.wait_ge(av_done, g * (NP // 4) + 2 * done[1])
                        project(bank[0], P * done[0], P * done[1])
                    if s < NQ:
                        scores(g, s)
                    if s >= LAG:
                        av(g, p0)
                    if s < LAG or late:
                        e_mm(where, g, "att", s + 4)
                    if s >= LAG:
                        av(g, p0 + 1)
                    if s < 2:
                        for j in range(4 * s, 4 * s + 4):
                            values(g, j)
                    if where == "loop":
                        if s == X_STEP:
                            x_turn(where, g, "att", g * 3 + 2)
                        if s == ROUTE_STEP:
                            route(where, g, "att", 0)
                        if s == W_STEP:
                            w_turn(where, g, "att", g * 2 + 1)
                if where == "loop":
                    next_ffn(2)
                pe.wait_ge(av_done, (g + 1) * (NP // 4))
                ins = project(acc, 0, GT) if where == "loop" else project(bank[0], GT - P, GT)
                ins.then_inc(z_full, 1)

            pe.wait_ge(const_ready, 8)
            pe.wait_ge(s_bias, 16 * (4 + len(STACK)))
            nc.tensor.transpose(misc[:, 0:NBIAS], raw_bias[0:NBIAS, :], ident[0:NBIAS, 0:NBIAS]).then_inc(misc_full, 1)
            x_turn("pro", 0, "route", 0)
            pe.wait_ge(split_lo, 1)
            route("pro", 0, "route", 0)
            uses = misc_use("pro", 0, "route", "x"), misc_use("pro", 0, "route", "w")
            ffn("pro", 0, 0, *uses, None, {2: [lambda: w_turn("pro", 0, "route", 0)],
                                              3: [lambda: w_wide("pro", 0, "route", 0), lambda: w_wide("pro", 0, "route", 1)]})
            back("pro", 0, "ffn2", "y", y_done, 1)
            x_turn("pro", 0, "ffn2", 1)
            pe.wait_ge(misc_done, misc_use("pro", 0, "ffn2", "x") + 1)
            pe.wait_ge(s_wp, 16)
            qkv("pro", 0, 0, 0)
            with pe.Fori(0, NGROUP - 1) as g:
                attention("loop", g)
                uses1 = misc_use("loop", g, "att", "x"), misc_use("loop", g, "att", "w")
                uses2 = misc_use("loop", g, "ffn1", "x"), misc_use("loop", g, "ffn1", "w")

                def next_chunk(c):
                    ffn("loop", g * 2 + 2, 1, *uses2, None, {}, range(c, c + 1))

                def first_q(i):
                    if i == 0:
                        pe.wait_ge(misc_done, misc_use("loop", g, "ffn2", "x") + 1)
                        pe.wait_ge(sg_ready, (g * 2 + 3) * NCH)
                    qkv("loop", g, g + 1, g * 2 + 2, range(i, i + 1))

                ffn("loop", g * 2 + 1, 0, *uses1, (z_done, g + 1),
                    {4: [lambda: back("loop", g, "ffn1", "z", z_done, g + 1)],
                     8: [lambda: x_turn("loop", g, "ffn1", g * 3 + 3)],
                     10: [lambda: route("loop", g, "ffn1", 1)],
                     15: [lambda: w_turn("loop", g, "ffn1", g * 2 + 2)],
                     NCH + 2: [lambda: next_chunk(0)],
                     NCH + 4: [lambda: next_chunk(1)]}, range(3, NCH + DLAG))
                ffn("loop", g * 2 + 2, 1, *uses2, (y_done, g * 2 + 2),
                    {3: [lambda: back("loop", g, "ffn2", "y", y_done, g * 2 + 2)],
                     7: [lambda: x_turn("loop", g, "ffn2", g * 3 + 4)],
                     NCH + 2: [lambda: first_q(0)],
                     NCH + 4: [lambda: first_q(1)]}, range(2, NCH + DLAG))
                qkv("loop", g, g + 1, g * 2 + 2, range(2, NQK))
            last = NGROUP - 1
            attention("last", last)
            back("last", last, "ffn1", "z", z_done, last + 1)
            x_turn("last", last, "ffn1", 3 * last + 2)
            route("last", last, "ffn1", 1)
            uses = misc_use("last", last, "ffn1", "x"), misc_use("last", last, "ffn1", "w")
            ffn("last", 2 * last + 1, 1, *uses, (z_done, last + 1),
                {2: [lambda: w_turn("last", last, "ffn1", 2 * last + 1)],
                 3: [lambda: w_wide("last", last, "ffn1", 0), lambda: w_wide("last", last, "ffn1", 1)]})
            back("last", last, "end", "y", y_done, 2 * last + 2)


_INS = ["L0_attn_X", "L0_attn_Wq", "L0_attn_bq", "L0_attn_Wk", "L0_attn_Wv", "L0_attn_Wproj", "L0_attn_bproj",
        "L0_attn_Wr", "L0_attn_br", "L0_attn_b_nd", "L0_ffn_W_router", "L0_ffn_W_gate", "L0_ffn_b_gate",
        "L0_ffn_W_up", "L0_ffn_b_up", "L0_ffn_W_out", "L0_ffn_b_out"]


def kernel(**inputs):
    import numpy as _np
    import concourse.bacc as _bacc
    from concourse import mybir as _mybir
    from concourse.bass_utils import run_bass_kernel_spmd as _run

    nc = _bacc.Bacc("TRN2", target_bir_lowering=False, num_devices=1, dynamic_dma_scratch_size=1024)
    arrays, args = {}, []
    for name in _INS:
        a = _np.asarray(inputs[name])
        if name == "L0_attn_X":
            a = a.reshape(T, D)
        if name == "L0_attn_b_nd":
            a = a[:, ::-1]
        a = _np.ascontiguousarray(a)
        arrays[f"in_{name}"] = a
        args.append(nc.dram_tensor(f"in_{name}", a.shape, _mybir.dt.from_np(a.dtype), kind="ExternalInput").ap())
    args.append(nc.dram_tensor("out_0", (T, D), _mybir.dt.float32, kind="ExternalOutput").ap())
    macaron(nc, *args)
    r = _run(nc, [arrays], core_ids=[0])
    return r.results[0]["out_0"].reshape(1, T, D)
```
